# Optimizing a Trainium2 kernel written in Bass

```python
import numpy as np
import jax
import jax.numpy as jnp

def _softmax(x, axis=-1):
    return jax.nn.softmax(x, axis=axis)

def _gelu(x):
    return jax.nn.gelu(x, approximate=True)

def _silu(x):
    return jax.nn.silu(x)

def _sigmoid(x):
    return jax.nn.sigmoid(x)

def _layernorm(x, axis=-1, eps=1e-05):
    m = jnp.mean(x, axis=axis, keepdims=True)
    v = jnp.var(x, axis=axis, keepdims=True)
    return (x - m) / jnp.sqrt(v + eps)

def _scatter_add(tgt, idx, src, axis=0):
    return tgt.at[idx].add(src)

def _segment_sum(src, seg, n):
    return jax.ops.segment_sum(src, seg, n)
kernel_name = 'mk_gnn_resnorm_d2_gnn_r8_3687d6'

def setup_inputs(seed: int=0):
    np.random.seed(seed)
    _w = jnp.asarray

    def _rec_inputs():
        import jax
        import jax.numpy as jnp
        _gk = jax.random.key(seed)
        x = -0.000202 + 1 * jax.random.normal(jax.random.fold_in(_gk, 1), (12500, 64), jnp.float32)
        src = jax.random.randint(jax.random.fold_in(_gk, 2), (200000,), 0, 12500, jnp.int32)
        dst = jnp.minimum((12500 * jax.random.uniform(jax.random.fold_in(_gk, 3), (200000,)) ** 2.0).astype(jnp.int32), 99999)
        _o = jnp.argsort(dst, stable=True)
        src = src[_o]
        dst = dst[_o]
        edge_attr_64 = -8.16379e-05 + 0.999858 * jax.random.normal(jax.random.fold_in(_gk, 12), (200000, 64), jnp.float32)
        edge_weight = jax.random.uniform(jax.random.fold_in(_gk, 14), (200000,), jnp.float32, 0.0, 1)
        return (x, src, dst, edge_attr_64, edge_weight)
    x, src, dst, edge_attr_64, edge_weight = _rec_inputs()

    def _L0_gnn_setup():
        import jax, jax.numpy as jnp
        import numpy as np
        N = 12500
        E = 400000
        D = 64
        K = 10
        ALPHA = 0.1
        key = jax.random.key(seed)
        k1, k2, k3, k4 = jax.random.split(key, 4)
        feat = jax.random.normal(k1, (N, D), dtype=jnp.float32)
        src = jax.random.randint(k2, (E,), 0, N, dtype=jnp.int32)
        dst = jax.random.randint(k3, (E,), 0, N, dtype=jnp.int32)
        edge_weight = jax.random.uniform(k4, (E,), dtype=jnp.float32)
        return {'feat': feat, 'edge_weight': edge_weight, 'src': src, 'dst': dst}
    _L0_gnn_all = _L0_gnn_setup()
    _L0_gnn_in = {k: v for k, v in _L0_gnn_all.items() if k in ()}
    del _L0_gnn_all

    def _L1_gnn_setup():
        import jax, jax.numpy as jnp
        import numpy as np
        N = 12500
        NE = 200000
        IN_DIM = 64
        OUT_DIM = 64
        H = 8
        D = OUT_DIM // H
        key = jax.random.key(seed)
        ks = jax.random.split(key, 12)
        s = 1.0 / np.sqrt(IN_DIM)
        x = jax.random.normal(ks[0], (N, IN_DIM), jnp.float32)
        edge_attr = jax.random.normal(ks[1], (NE, IN_DIM), jnp.float32)
        edge_index = jax.random.randint(ks[2], (2, NE), 0, N, dtype=jnp.int32)
        WQ = jax.random.normal(ks[3], (IN_DIM, OUT_DIM), jnp.float32) * s
        WK = jax.random.normal(ks[4], (IN_DIM, OUT_DIM), jnp.float32) * s
        WE = jax.random.normal(ks[5], (IN_DIM, OUT_DIM), jnp.float32) * s
        WV = jax.random.normal(ks[6], (IN_DIM, OUT_DIM), jnp.float32) * s
        bQ = jax.random.normal(ks[7], (OUT_DIM,), jnp.float32) * 0.01
        bK = jax.random.normal(ks[8], (OUT_DIM,), jnp.float32) * 0.01
        bE = jax.random.normal(ks[9], (OUT_DIM,), jnp.float32) * 0.01
        bV = jax.random.normal(ks[10], (OUT_DIM,), jnp.float32) * 0.01
        return {'x': x, 'edge_attr': edge_attr, 'edge_index': edge_index, 'WQ': WQ, 'bQ': bQ, 'WK': WK, 'bK': bK, 'WE': WE, 'bE': bE, 'WV': WV, 'bV': bV}
    _L1_gnn_all = _L1_gnn_setup()
    _L1_gnn_in = {k: v for k, v in _L1_gnn_all.items() if k in ('WQ', 'bQ', 'WK', 'bK', 'WE', 'bE', 'WV', 'bV')}
    del _L1_gnn_all
    return {'x': x, 'src': src, 'dst': dst, 'edge_attr_64': edge_attr_64, 'edge_weight': edge_weight, 'L1_gnn_WQ': _L1_gnn_in['WQ'], 'L1_gnn_bQ': _L1_gnn_in['bQ'], 'L1_gnn_WK': _L1_gnn_in['WK'], 'L1_gnn_bK': _L1_gnn_in['bK'], 'L1_gnn_WE': _L1_gnn_in['WE'], 'L1_gnn_bE': _L1_gnn_in['bE'], 'L1_gnn_WV': _L1_gnn_in['WV'], 'L1_gnn_bV': _L1_gnn_in['bV']}

def reference(x, src, dst, edge_attr_64, edge_weight, L1_gnn_WQ, L1_gnn_bQ, L1_gnn_WK, L1_gnn_bK, L1_gnn_WE, L1_gnn_bE, L1_gnn_WV, L1_gnn_bV):
    import jax
    import jax.numpy as jnp

    def _L0_gnn_ref(feat, edge_weight, src, dst):
        import jax, jax.numpy as jnp
        import numpy as np
        N = 12500
        E = 400000
        D = 64
        K = 10
        ALPHA = 0.1
        n = feat.shape[0]
        loop = jnp.arange(n, dtype=src.dtype)
        s = jnp.concatenate([src, loop])
        d = jnp.concatenate([dst, loop])
        w = jnp.concatenate([edge_weight, jnp.ones((n,), feat.dtype)])
        deg_out = jax.ops.segment_sum(w, s, num_segments=n)
        deg_in = jax.ops.segment_sum(w, d, num_segments=n)
        inv_sqrt_out = jnp.where(deg_out > 0, jax.lax.rsqrt(deg_out), 0.0)
        inv_sqrt_in = jnp.where(deg_in > 0, jax.lax.rsqrt(deg_in), 0.0)
        wn = w * inv_sqrt_out[s] * inv_sqrt_in[d]
        feat_0 = feat

        def step(h, _):
            agg = jax.ops.segment_sum(h[s] * wn[:, None], d, num_segments=n)
            return ((1.0 - ALPHA) * agg + ALPHA * feat_0, None)
        h, _ = jax.lax.scan(step, feat, None, length=K)
        return h

    def _L1_gnn_ref(x, edge_attr, edge_index, WQ, bQ, WK, bK, WE, bE, WV, bV):
        import jax, jax.numpy as jnp
        import numpy as np
        N = 12500
        NE = 200000
        IN_DIM = 64
        OUT_DIM = 64
        H = 8
        D = OUT_DIM // H
        n = x.shape[0]
        Qh = (x @ WQ + bQ).reshape(n, H, D)
        Kh = (x @ WK + bK).reshape(n, H, D)
        Vh = (x @ WV + bV).reshape(n, H, D)
        Eh = (edge_attr @ WE + bE).reshape(-1, H, D)
        src = edge_index[0]
        dst = edge_index[1]
        inv_sqrt_d = jnp.float32(1.0 / np.sqrt(D))
        score = Kh[src] * Qh[dst] * inv_sqrt_d * Eh
        score = jnp.exp(jnp.clip(score.sum(-1, keepdims=True), -5.0, 5.0))
        msg = Vh[src] * score
        wV = jax.ops.segment_sum(msg, dst, num_segments=n)
        return wV.reshape(n, H * D)
    edge_index = jnp.stack([src, dst])
    x = _layernorm(x + _L0_gnn_ref(x, edge_weight, src, dst), axis=-1)
    x = _layernorm(x + _L1_gnn_ref(x, edge_attr_64, edge_index, L1_gnn_WQ, L1_gnn_bQ, L1_gnn_WK, L1_gnn_bK, L1_gnn_WE, L1_gnn_bE, L1_gnn_WV, L1_gnn_bV), axis=-1)
    return x

_drawn_inputs = setup_inputs


def setup_inputs(seed=0):
    import zlib

    import numpy as np

    out = dict(_drawn_inputs(seed))
    spreads = {}
    factors = {'L1_gnn_bQ': 5.164, 'L1_gnn_bK': 5.367, 'L1_gnn_bE': 4.801}
    for name, (base, spread) in spreads.items():
        noise = np.random.default_rng([zlib.crc32(name.encode()), seed]).standard_normal(out[name].shape)
        drawn = base * np.exp(spread * noise) if base else spread * noise
        out[name] = jnp.asarray(drawn.astype(out[name].dtype))
    for name, factor in factors.items():
        out[name] = (out[name] * factor).astype(out[name].dtype)
    return out
```

```python
from contextlib import ExitStack

import concourse.bass as bass
from concourse import mybir

F32 = mybir.dt.float32
BF16 = mybir.dt.bfloat16
I32 = mybir.dt.int32
U32 = mybir.dt.uint32
ALU = mybir.AluOpType
ACT = mybir.ActivationFunctionType
AX = mybir.AxisListType.X

P = 128
STEPS = 10
ALPHA = 0.1
EPS = 1e-5
HEADS = 8
GT = 4
GE = GT * P
CG = 4
CT = CG * GT
CE = CG * GE
NB = 7
ROUND = 12582912.0


class Chain:

    def __init__(self, eng, sem, base=0):
        self.eng, self.sem, self.base, self.n = eng, sem, base, 0

    def __call__(self, ins):
        self.n += 1
        ins.then_inc(self.sem, 1)
        self.eng.wait_ge(self.sem, self.base + self.n)


def build(nc, x, src, dst, edge_attr, edge_weight, WQ, bQ, WK, bK, WE, bE, WV, bV, out):
    N, D = x.shape
    E = src.shape[0]
    DH = D // HEADS
    NJ = -(-N // P)
    assert NJ % (2 * NB) == 0 and D == 64 and DH * HEADS == D
    NT = P * NJ
    NCH = -(-E // CE)
    assert NCH % 2 == 0
    PAIRS = NCH // 2
    EP = NCH * CE
    NQ = EP // GE
    QB = -(-NQ // P)
    NT_TILES = NQ * GT
    WRAP = 2 * CG
    NODE_PAIRS = NJ // (2 * NB)
    NODE_BLOCKS = 2 * NODE_PAIRS
    PARTS = 2
    PART_STEPS = STEPS // PARTS
    assert PART_STEPS * PARTS == STEPS and PART_STEPS * PAIRS * 16 * CT < 65536
    ZERO_ROW = EP
    QF = E // GE
    REST = E - QF * GE

    node_rows = nc.dram_tensor("node_rows", [NT, D], F32).ap()
    edge_rows = nc.dram_tensor("edge_rows", [EP + P, D], F32).ap()
    same_rows = nc.dram_tensor("same_rows", [(NQ + WRAP) * GE], BF16).ap()
    attr_rows = nc.dram_tensor("attr_rows", [EP, D], F32).ap()
    kv_rows = nc.dram_tensor("kv_rows", [NT, 2 * D], F32).ap()
    q_rows = nc.dram_tensor("q_rows", [NT, D], F32).ap()

    node_rows_v = node_rows.rearrange("(p j) f -> p (j f)", j=NJ)
    kv_rows_v = kv_rows.rearrange("(p j) f -> p j f", j=NJ)
    q_rows_v = q_rows.rearrange("(p j) f -> p j f", j=NJ)
    edge_rows_v = edge_rows[0:EP, :].rearrange("(g p u) f -> p g (u f)", p=P, u=GT)
    attr_rows_v = attr_rows.rearrange("(g p u) f -> p g (u f)", p=P, u=GT)

    with ExitStack() as ctx:
        def sb(name, shape, dt=F32):
            return ctx.enter_context(nc.sbuf_tensor(name, shape, dt))

        def sem(name):
            return ctx.enter_context(nc.semaphore(name))

        x_sb = sb("x_sb", [P, NJ * D])
        h_sb = sb("h_sb", [P, NJ * D])
        u_sb = sb("u_sb", [P, NJ * D])
        tmp = sb("tmp", [P, NJ * D])
        src_idx = sb("src_idx", [P, (NQ + WRAP) * GT], I32)
        dst_idx = sb("dst_idx", [P, (NQ + WRAP) * GT], I32)
        w_p = sb("w_p", [P, (NQ + WRAP) * GT])
        end_idx = sb("end_idx", [P, NJ + 2 * NB], I32)
        rows_in = sb("rows_in", [P, 2, CT, D])
        scaled = sb("scaled", [P, 2, CT, D])
        sums = sb("sums", [P, 2, CE])
        same = sb("same", [D, 2, CE], BF16)
        rows_out = sb("rows_out", [P, 2, CT, D])
        src_st = sb("src_st", [P, 2, CT], I32)
        dst_st = sb("dst_st", [P, 2, CT], I32)
        w_st = sb("w_st", [P, 2, CT])
        end_st = sb("end_st", [P, 2, NB], I32)
        ends_in = sb("ends_in", [P, 2, NB, D])
        ident = sb("ident", [P, P])
        lower = sb("lower", [P, P])
        iota_p = sb("iota_p", [P, P])
        iota_j = sb("iota_j", [P, NJ])
        ones = sb("ones", [P, NJ])
        zeros = sb("zeros", [P, 2 * NJ])
        inv_out = sb("inv_out", [P, NJ])
        inv_in9 = sb("inv_in9", [P, NJ])
        deg = sb("deg", [P, 3, NJ])
        deg_t = sb("deg_t", [P, 3, NJ])
        count = sb("count", [P, NJ])
        first = sb("first", [P, 1])
        w_kvq = sb("w_kvq", [D + 1, 3 * D])
        w_e = sb("w_e", [D + 1, D])
        stat = sb("stat", [P, 2, NJ])
        score = sb("score", [P, 2, GT, HEADS])

        nat_i = tmp[:, 0:3 * QB * GE].rearrange("p (a r i) -> p a r i", a=3, i=GE)
        src_nat, dst_nat = nat_i[:, 0].bitcast(I32), nat_i[:, 1].bitcast(I32)
        w_nat = nat_i[:, 2]
        nat_f = u_sb[:, 0:3 * QB * GE].rearrange("p (a r i) -> p a r i", a=3, i=GE)
        prev_nat, dst_f, prev_f = nat_f[:, 0].bitcast(I32), nat_f[:, 1], nat_f[:, 2]
        src_f = sums[:, :, :].rearrange("p a e -> p (a e)")[:, 0:QB * GE].rearrange("p (r i) -> p r i", i=GE)
        same_nat = x_sb[:, 0:QB * GE // 2].bitcast(BF16).rearrange("p (r i) -> p r i", i=GE)
        src_pf = rows_in[:, :, :, :].rearrange("p a t f -> p (a t f)")[:, 0:NT_TILES]
        dst_pf = scaled[:, :, :, :].rearrange("p a t f -> p (a t f)")[:, 0:NT_TILES]
        digits = tmp[:, 0:4 * NT_TILES].rearrange("p (a t) -> p a t", a=4)
        src_hi, src_lo, dst_hi, dst_lo = (digits[:, a] for a in range(4))
        HOT = 2 * P + 3 * NJ
        HB = 4
        hots = h_sb[:, 0:2 * HB * HOT].rearrange("p (b t c) -> p b t c", b=2, c=HOT)

        kvq_out = tmp[:, 0:2 * NB * 3 * D].rearrange("p (b j f) -> p b j f", b=2, f=3 * D)
        x_st = tmp[:, 2 * NB * 3 * D:2 * NB * 4 * D].rearrange("p (b j f) -> p b j f", b=2, f=D)
        xT = u_sb[0:D + 1, 0:2 * NB * P].rearrange("p (b j n) -> p b j n", b=2, n=P)
        kv_in = u_sb[:, 0:2 * CT * 2 * D].rearrange("p (b t f) -> p b t f", b=2, f=2 * D)
        attrT = u_sb[0:D + 1, 2 * CT * 2 * D:2 * CT * 2 * D + 2 * GE].rearrange("p (b e) -> p b e", b=2)
        attr_in = tmp[:, 0:2 * CT * D].rearrange("p (b t f) -> p b t f", b=2, f=D)
        prod = tmp[:, 2 * CT * D:2 * CT * D + 2 * GT * D].rearrange("p (b t f) -> p b t f", b=2, f=D)
        msg = tmp[:, 2 * CT * D + 2 * GT * D:2 * CT * D + 6 * GT * D].rearrange("p (b t f) -> p b t f", b=4, f=D)

        fwd = ctx.enter_context(nc.psum_tensor("fwd", [P, 4, GE], F32))
        back = ctx.enter_context(nc.psum_tensor("back", [P, 2, GE], F32))
        proj = ctx.enter_context(nc.psum_tensor("proj", [P, 2, GE], F32))

        loaded_e = sem("loaded_e")
        loaded_x = sem("loaded_x")
        loaded_w = sem("loaded_w")
        attr_copied = sem("attr_copied")
        cleared = sem("cleared")
        consts = sem("consts")
        vec_pre = sem("vec_pre")
        vec_node = sem("vec_node")
        vec_ln = sem("vec_ln")
        vec_edge = sem("vec_edge")
        nat_ready = sem("nat_ready")
        same_nat_ready = sem("same_nat_ready")
        same_stored = sem("same_stored")
        nat_T = sem("nat_T")
        nat_T_used = sem("nat_T_used")
        hots_ready = sem("hots_ready")
        hots_used = sem("hots_used")
        counted = sem("counted")
        root_in = sem("root_in")
        root_done = sem("root_done")
        totals_ready = sem("totals_ready")
        offsets_ready = sem("offsets_ready")
        node_init = sem("node_init")
        staged = sem("staged")
        end_staged = sem("end_staged")
        gathered = [[sem(f"gathered{part}_{b}") for b in range(2)] for part in range(PARTS + 1)]
        scaled_done = sem("scaled_done")
        fwd_done = sem("fwd_done")
        same_ready = [sem("same_ready0"), sem("same_ready1")]
        scan_done = sem("scan_done")
        back_done = sem("back_done")
        out_copied = sem("out_copied")
        rows_stored = [sem("rows_stored0"), sem("rows_stored1")]
        ends_gathered = [sem("ends_gathered0"), sem("ends_gathered1")]
        node_done = sem("node_done")
        node_stored = sem("node_stored")
        x1_staged = sem("x1_staged")
        x1T_done = sem("x1T_done")
        x1T_copied = sem("x1T_copied")
        kvq_done = sem("kvq_done")
        kvq_copied = sem("kvq_copied")
        kvq_stored = [sem("kvq_stored0"), sem("kvq_stored1")]
        ones_row = sem("ones_row")
        attr_loaded = [sem("attr_loaded0"), sem("attr_loaded1")]
        attrT_done = sem("attrT_done")
        attrT_copied = sem("attrT_copied")
        eproj_done = sem("eproj_done")
        clipped = sem("clipped")
        exp_done = sem("exp_done")
        msg_done = sem("msg_done")
        msg_ready = sem("msg_ready")
        kv_used = sem("kv_used")
        y_done = sem("y_done")
        y_stored = sem("y_stored")
        passed = sem("passed")

        def wait_count(eng, sem, count):
            eng.wait_ge(sem, count)
            eng.sem_inc(passed, 1)

        FREE_G = 2 * CG
        FREE_F = 4
        FREE_B = 2

        block = ctx.enter_context(nc.Block())

        @block.sync
        def _(sp):
            sp.wait_ge(cleared, 1)
            for a, nat in ((src, src_nat), (dst, dst_nat), (edge_weight, w_nat)):
                full = (QB - 1) * P
                sp.dma_start(nat[:, 0:QB - 1, :], a[0:full * GE].rearrange("(r p i) -> p r i", p=P, i=GE)).then_inc(loaded_e, 16)
                sp.dma_start(nat[0:QF - full, QB - 1, :], a[full * GE:QF * GE].rearrange("(p i) -> p i", i=GE)).then_inc(loaded_e, 16)
                sp.dma_start(nat[QF - full:QF - full + 1, QB - 1, 0:REST], a[QF * GE:E].rearrange("(p i) -> p i", p=1)).then_inc(loaded_e, 16)
            full = (QB - 1) * P
            sp.dma_start(prev_nat[0:1, 0, 1:GE], dst[0:GE - 1].rearrange("(p i) -> p i", p=1)).then_inc(loaded_e, 16)
            sp.dma_start(prev_nat[1:P, 0, :], dst[GE - 1:P * GE - 1].rearrange("(p i) -> p i", i=GE)).then_inc(loaded_e, 16)
            sp.dma_start(prev_nat[:, 1:QB - 1, :], dst[P * GE - 1:full * GE - 1].rearrange("(r p i) -> p r i", p=P, i=GE)).then_inc(loaded_e, 16)
            sp.dma_start(prev_nat[0:QF - full, QB - 1, :], dst[full * GE - 1:QF * GE - 1].rearrange("(p i) -> p i", i=GE)).then_inc(loaded_e, 16)
            sp.dma_start(prev_nat[QF - full:QF - full + 1, QB - 1, 0:REST], dst[QF * GE - 1:E - 1].rearrange("(p i) -> p i", p=1)).then_inc(loaded_e, 16)
            sp.dma_start(w_kvq[0:D, 0:D], WK).then_inc(loaded_w, 16)
            sp.dma_start(w_kvq[0:D, D:2 * D], WV).then_inc(loaded_w, 16)
            sp.dma_start(w_kvq[0:D, 2 * D:3 * D], WQ).then_inc(loaded_w, 16)
            sp.dma_start(w_e[0:D, :], WE).then_inc(loaded_w, 16)
            for b, to in ((bK, w_kvq[D:D + 1, 0:D]), (bV, w_kvq[D:D + 1, D:2 * D]), (bQ, w_kvq[D:D + 1, 2 * D:3 * D]), (bE, w_e[D:D + 1, :])):
                sp.dma_start(to, b.rearrange("(p f) -> p f", p=1)).then_inc(loaded_w, 16)
            sp.wait_ge(consts, 1)
            for b in range(2):
                sp.dma_start(edge_rows[EP + 64 * b:EP + 64 * b + 64, :], zeros[0:64, 0:D]).then_inc(rows_stored[b], 16)
            half = E // 32 * 16
            sp.dma_start(attr_rows[0:half, :].rearrange("(a b) f -> a (b f)", a=16), edge_attr[0:half, :].rearrange("(a b) f -> a (b f)", a=16)).then_inc(attr_copied, 16)
            sp.dma_start(attr_rows[half:E, :].rearrange("(a b) f -> a (b f)", a=16), edge_attr[half:E, :].rearrange("(a b) f -> a (b f)", a=16)).then_inc(attr_copied, 16)
            for r0 in range(E, EP, 64):
                sp.dma_start(attr_rows[r0:r0 + 64, :], zeros[0:64, 0:D]).then_inc(attr_copied, 16)
            sp.wait_ge(same_nat_ready, 1)
            full = (QB - 1) * P
            sp.dma_start(same_rows[0:full * GE].rearrange("(r p i) -> p r i", p=P, i=GE), same_nat[:, 0:QB - 1, :]).then_inc(same_stored, 16)
            sp.dma_start(same_rows[full * GE:NQ * GE].rearrange("(p i) -> p i", i=GE), same_nat[0:NQ - full, QB - 1, :]).then_inc(same_stored, 16)
            sp.dma_start(same_rows[NQ * GE:(NQ + WRAP) * GE].rearrange("(p i) -> p i", i=GE), same_nat[0:WRAP, 0, :]).then_inc(same_stored, 16)
            sp.wait_ge(same_stored, 48)
            for b in range(2):
                sp.dma_start(same[:, b, :], same_rows[b * CE:(b + 1) * CE].partition_broadcast(D)).then_inc(same_ready[b], 16)
            sp.wait_ge(cleared, 2)
            for p0, p1 in ((0, 112), (112, P - 1)):
                sp.dma_start(x_sb[p0:p1, :], x[p0 * NJ:p1 * NJ, :].rearrange("(p j) f -> p (j f)", j=NJ)).then_inc(loaded_x, 16)
            sp.dma_start(x_sb[P - 1:P, 0:(N - (P - 1) * NJ) * D], x[(P - 1) * NJ:N, :].rearrange("(p j) f -> p (j f)", p=1)).then_inc(loaded_x, 16)
            sp.wait_ge(node_init, 1)
            sp.dma_start(node_rows_v, u_sb[:, :]).then_inc(node_stored, 16 * NODE_BLOCKS)

            def edge_pass(q, i):
                for b in range(2):
                    c = q * 2 + b
                    sp.wait_ge(scan_done, c * CG + CG + FREE_F)
                    sp.dma_start(same[:, b, :], same_rows[bass.ds(i * (2 * CE) + (b + 2) * CE, CE)].partition_broadcast(D)).then_inc(same_ready[b], 16)
                    sp.wait_ge(out_copied, c * CG + CG + FREE_B)
                    sp.dma_start(edge_rows_v[:, bass.ds(i * (2 * CG) + b * CG, CG), :],
                                 rows_out[:, b, :, :].rearrange("p (g u) f -> p g (u f)", u=GT)).then_inc(rows_stored[b], 16)

            for part in range(PARTS):
                with sp.Fori(0, PART_STEPS) as kk:
                    k = kk + part * PART_STEPS
                    with sp.Fori(0, PAIRS) as i:
                        edge_pass(k * PAIRS + i, i)
                    with sp.Fori(0, NODE_PAIRS) as j:
                        for b in range(2):
                            n = (k * NODE_PAIRS + j) * 2 + b
                            sp.wait_ge(node_done, n + 1 + 2)
                            cols = bass.ds((j * 2 + b) * (NB * D), NB * D)
                            sp.dma_start(node_rows_v[:, cols], u_sb[:, cols]).then_inc(node_stored, 16)

            with sp.Fori(0, NODE_PAIRS) as j:
                for b in range(2):
                    n = j * 2 + b
                    sp.wait_ge(kvq_copied, n + 1)
                    sp.dma_start(kv_rows_v[:, bass.ds(n * NB, NB), :], kvq_out[:, b, :, 0:2 * D]).then_inc(kvq_stored[b], 16)
                    sp.dma_start(q_rows_v[:, bass.ds(n * NB, NB), :], kvq_out[:, b, :, 2 * D:3 * D]).then_inc(kvq_stored[b], 16)
            for b in range(2):
                sp.wait_ge(kvq_stored[b], 32 * NODE_PAIRS)
            sp.wait_ge(attr_copied, 16 * (2 + (EP - E) // 64))
            for b in range(2):
                sp.dma_start(attr_in[:, b, :, :].rearrange("p (g u) f -> p g (u f)", u=GT),
                             attr_rows_v[:, b * CG:(b + 1) * CG, :]).then_inc(attr_loaded[b], 16)

            def attr_load(i, b):
                sp.wait_ge(attrT_done, (i * 2 + b + 1) * CG + 2)
                sp.dma_start(attr_in[:, b, :, :].rearrange("p (g u) f -> p g (u f)", u=GT),
                             attr_rows_v[:, bass.ds(i * (2 * CG) + (b + 2) * CG, CG), :]).then_inc(attr_loaded[b], 16)

            with sp.Fori(0, PAIRS - 1) as i:
                for b in range(2):
                    attr_load(i, b)
                edge_pass(i + STEPS * PAIRS, i)
            edge_pass(STEPS * PAIRS + PAIRS - 1, PAIRS - 1)
            sp.wait_ge(y_done, 1)
            for p0, p1 in ((0, 112), (112, P - 1)):
                sp.dma_start(out[p0 * NJ:p1 * NJ, :].rearrange("(p j) f -> p (j f)", j=NJ), h_sb[p0:p1, :]).then_inc(y_stored, 16)
            sp.dma_start(out[(P - 1) * NJ:N, :].rearrange("(p j) f -> p (j f)", p=1), h_sb[P - 1:P, 0:(N - (P - 1) * NJ) * D]).then_inc(y_stored, 16)
            sp.wait_ge(y_stored, 48)
            for b in range(2):
                sp.wait_ge(same_ready[b], 16 * (1 + (STEPS + 1) * PAIRS))

        @block.gpsimd
        def _(pool):
            g = nc.gpsimd
            pool.memset(zeros[:, :], 0.0).then_inc(consts, 1)
            pool.memset(ident[:, :], 0.0)
            pool.memset(lower[:, :], 1.0)
            pool.iota(iota_p[:, :], pattern=[[1, P]], base=0, channel_multiplier=0, allow_small_or_imprecise_dtypes=True)
            pool.iota(iota_j[:, :], pattern=[[1, NJ]], base=0, channel_multiplier=0, allow_small_or_imprecise_dtypes=True)
            pool.memset(ones[:, :], 1.0).then_inc(consts, 1)
            pool.wait_ge(consts, 2)
            pool.affine_select(out=ident[:, :], in_=ident[:, :], compare_op=ALU.not_equal, fill=1.0, base=0,
                               pattern=[[-1, P]], channel_multiplier=1)
            pool.affine_select(out=lower[:, :], in_=lower[:, :], compare_op=ALU.is_gt, fill=0.0, base=0,
                               pattern=[[1, P]], channel_multiplier=-1).then_inc(consts, 1)

            for part in range(PARTS):
                with pool.Fori(0, PART_STEPS) as kk:
                    k = kk + part * PART_STEPS
                    wait_count(pool, node_stored, (k + 1) * (16 * NODE_BLOCKS))
                    with pool.Fori(0, PAIRS) as i:
                        for b in range(2):
                            c = (k * PAIRS + i) * 2 + b
                            wait_count(pool, staged, c + 1)
                            wait_count(pool, scaled_done, c * CG + CG)
                            for t in range(CT):
                                g.indirect_dma_start(out=rows_in[:, b, t, :], out_offset=None, in_=node_rows,
                                                     in_offset=bass.IndirectOffsetOnAxis(ap=src_st[:, b, t:t + 1].bitcast(U32), axis=0)).then_inc(gathered[part][b], 16)
                    for b in range(2):
                        wait_count(pool, rows_stored[b], (k + 1) * (16 * PAIRS) + 16)
                    with pool.Fori(0, NODE_PAIRS) as j:
                        for b in range(2):
                            n = (k * NODE_PAIRS + j) * 2 + b
                            wait_count(pool, end_staged, n + 1)
                            wait_count(pool, node_done, n + 1)
                            for t in range(NB):
                                g.indirect_dma_start(out=ends_in[:, b, t, :], out_offset=None, in_=edge_rows,
                                                     in_offset=bass.IndirectOffsetOnAxis(ap=end_st[:, b, t:t + 1].bitcast(U32), axis=0)).then_inc(ends_gathered[b], 16)

            for b in range(2):
                pool.wait_ge(kvq_stored[b], 32 * NODE_PAIRS)
            with pool.Fori(0, PAIRS) as i:
                for b in range(2):
                    c = (i + STEPS * PAIRS) * 2 + b
                    wait_count(pool, staged, c + 1)
                    wait_count(pool, kv_used, (i * 2 + b + 1) * CG)
                    for t in range(CT):
                        g.indirect_dma_start(out=kv_in[:, b, t, :], out_offset=None, in_=kv_rows,
                                             in_offset=bass.IndirectOffsetOnAxis(ap=src_st[:, b, t:t + 1].bitcast(U32), axis=0)).then_inc(gathered[PARTS][b], 16)
                        g.indirect_dma_start(out=rows_in[:, b, t, :], out_offset=None, in_=q_rows,
                                             in_offset=bass.IndirectOffsetOnAxis(ap=dst_st[:, b, t:t + 1].bitcast(U32), axis=0)).then_inc(gathered[PARTS][b], 16)
            for b in range(2):
                pool.wait_ge(rows_stored[b], (STEPS + 1) * (16 * PAIRS) + 16)
            with pool.Fori(0, NODE_PAIRS) as j:
                for b in range(2):
                    n = (j + STEPS * NODE_PAIRS) * 2 + b
                    wait_count(pool, end_staged, n + 1)
                    wait_count(pool, node_done, n + 1)
                    for t in range(NB):
                        g.indirect_dma_start(out=ends_in[:, b, t, :], out_offset=None, in_=edge_rows,
                                             in_offset=bass.IndirectOffsetOnAxis(ap=end_st[:, b, t:t + 1].bitcast(U32), axis=0)).then_inc(ends_gathered[b], 16)

        @block.scalar
        def _(act):
            act.sem_inc(scaled_done, FREE_G)
            act.sem_inc(out_copied, FREE_B)
            act.wait_ge(root_in, 1)
            nc.scalar.activation(deg_t[:, 0:2, :], deg[:, 0:2, :], ACT.Sqrt).then_inc(root_done, 1)

            def copy_out(q, b, g):
                G = (q * 2 + b) * CG + g
                act.wait_ge(back_done, G + 1 + FREE_G)
                if g == 0:
                    act.wait_ge(rows_stored[b], q * 16 + 16)
                nc.scalar.activation(rows_out[:, b, g * GT:(g + 1) * GT, :], back[:, g % 2, 0:GT * D].rearrange("p (t f) -> p t f", f=D), ACT.Copy).then_inc(out_copied, 1)

            for part in range(PARTS):
                with act.Fori(0, PART_STEPS) as kk:
                    k = kk + part * PART_STEPS
                    with act.Fori(0, PAIRS) as i:
                        q = k * PAIRS + i
                        for b in range(2):
                            act.wait_ge(gathered[part][b], (kk * PAIRS + i + 1) * (16 * CT))
                            act.wait_ge(fwd_done, (q * 2 + b) * CG + CG)
                            for g in range(CG):
                                for t in range(g * GT, (g + 1) * GT):
                                    last = nc.scalar.activation(scaled[:, b, t, :], rows_in[:, b, t, :], ACT.Copy, scale=w_st[:, b, t:t + 1])
                                last.then_inc(scaled_done, 1)
                            for g in range(CG):
                                copy_out(q, b, g)
            act.wait_ge(root_in, 2)
            nc.scalar.activation(stat[:, 0, :], stat[:, 1, :], ACT.Sqrt).then_inc(root_done, 1)
            with act.Fori(0, NODE_PAIRS) as j:
                for b in range(2):
                    n = j * 2 + b
                    act.wait_ge(x1T_done, n + 1)
                    act.wait_ge(kvq_done, n + 1)
                    nc.scalar.activation(xT[0:D, b, :, :].rearrange("p j n -> p (j n)"), proj[0:D, :, :].rearrange("p b e -> p (b e)")[:, 0:NB * P], ACT.Copy).then_inc(x1T_copied, 1)

            def attr_copy(G, g):
                act.wait_ge(attrT_done, G + 1 + 2)
                act.wait_ge(eproj_done, G + 1)
                nc.scalar.activation(attrT[0:D, g % 2, :], fwd[0:D, g % 2, :], ACT.Copy).then_inc(attrT_copied, 1)

            with act.Fori(0, PAIRS) as i:
                q = i + STEPS * PAIRS
                attr_copy(i * (2 * CG), 0)
                for g in range(2 * CG):
                    G = i * (2 * CG) + g
                    if g + 1 < 2 * CG:
                        attr_copy(G + 1, g + 1)
                    act.wait_ge(clipped, G + 1)
                    nc.scalar.activation(score[:, g % 2, :, :], score[:, g % 2, :, :], ACT.Exp).then_inc(exp_done, 1)
                    copy_out(q, g // CG, g % CG)
            act.wait_ge(root_in, 3)
            nc.scalar.activation(stat[:, 0, :], stat[:, 1, :], ACT.Sqrt).then_inc(root_done, 1)

        @block.vector
        def _(dve):
            v = nc.vector
            link = Chain(dve, vec_pre)
            dve.sem_inc(scan_done, FREE_F)
            dve.sem_inc(node_done, 2)
            v.memset(dst_nat[:, QB - 1, :], NT)
            v.memset(src_nat[:, QB - 1, :], 0)
            v.memset(w_nat[:, QB - 1, :], 0.0)
            v.memset(prev_nat[:, QB - 1, :], 0)
            v.memset(h_sb[:, :], 0.0)
            link(v.memset(prev_nat[0:1, 0, 0:1], -1))
            v.memset(sums[:, 1, :], 0.0).then_inc(cleared, 1)
            dve.wait_ge(loaded_e, 16 * 14)
            v.tensor_copy(dst_f, dst_nat)
            v.tensor_copy(prev_f, prev_nat)
            link(v.tensor_copy(src_f, src_nat))
            dve.sem_inc(nat_ready, 1)
            v.tensor_tensor(same_nat, dst_f, prev_f, ALU.is_equal).then_inc(same_nat_ready, 1)
            n = 0
            for a, to in ((0, src_pf), (1, dst_pf), (2, w_p[:, 0:NT_TILES])):
                to_v = to.rearrange("p (q u) -> p u q", u=GT)
                for r in range(QB):
                    rows = min(P, NQ - r * P)
                    dve.wait_ge(nat_T, n + 1)
                    link(v.tensor_copy(to_v[:, :, r * P:r * P + rows], fwd[:, n % 4, :].rearrange("p (u q) -> p u q", u=GT)[:, :, 0:rows]))
                    dve.sem_inc(nat_T_used, 1)
                    n += 1
            v.tensor_copy(src_idx[:, 0:NT_TILES], src_pf)
            link(v.tensor_scalar(dst_idx[:, 0:NT_TILES], dst_pf, float(NT - 1), None, ALU.min))
            W = WRAP * GT
            v.tensor_copy(src_idx[:, NT_TILES:NT_TILES + W], src_idx[:, 0:W])
            v.tensor_copy(dst_idx[:, NT_TILES:NT_TILES + W], dst_idx[:, 0:W])
            link(v.tensor_copy(w_p[:, NT_TILES:NT_TILES + W], w_p[:, 0:W]))
            for f, hi, lo in ((src_pf, src_hi, src_lo), (dst_pf, dst_hi, dst_lo)):
                link(v.tensor_scalar(hi, f, 1.0 / NJ, 0.5 / NJ - 0.5, ALU.mult, ALU.add))
                link(v.tensor_scalar(hi, hi, ROUND, None, ALU.add))
                link(v.tensor_scalar(hi, hi, ROUND, None, ALU.subtract))
                link(v.scalar_tensor_tensor(lo, hi, -float(NJ), f, ALU.mult, ALU.add))
            dve.wait_ge(same_stored, 48)
            link(v.memset(x_sb[96:P, :], 0.0))
            dve.sem_inc(cleared, 1)
            with dve.Fori(0, NT_TILES // (2 * HB)) as i:
                for b in range(2):
                    dve.wait_ge(hots_used, i * 2 + b + 1)
                    for t in range(HB):
                        at = bass.ds(i * (2 * HB) + (b * HB + t), 1)
                        o = hots[:, b, t, :]
                        v.tensor_scalar(o[:, 0:P], iota_p[:, :], dst_hi[:, at], None, ALU.is_equal)
                        v.tensor_scalar(o[:, P:P + NJ], iota_j[:, :], dst_lo[:, at], w_p[:, at], ALU.is_equal, ALU.mult)
                        v.tensor_scalar(o[:, P + NJ:P + 2 * NJ], iota_j[:, :], dst_lo[:, at], None, ALU.is_equal)
                        v.tensor_scalar(o[:, P + 2 * NJ:2 * P + 2 * NJ], iota_p[:, :], src_hi[:, at], None, ALU.is_equal)
                        last = v.tensor_scalar(o[:, 2 * P + 2 * NJ:HOT], iota_j[:, :], src_lo[:, at], w_p[:, at], ALU.is_equal, ALU.mult)
                    last.then_inc(hots_ready, 1)
            dve.wait_ge(counted, 1)
            v.tensor_scalar(deg[:, 1, :], back[:, 0, 0:NJ], 1.0, None, ALU.add)
            v.tensor_copy(count[:, :], back[:, 0, NJ:2 * NJ])
            link(v.tensor_scalar(deg[:, 0, :], back[:, 1, 0:NJ], 1.0, None, ALU.add))
            v.tensor_scalar(inv_out[:, :], deg[:, 0, :], 0.0, None, ALU.is_gt)
            link(v.tensor_scalar(inv_in9[:, :], deg[:, 1, :], 0.0, 1.0 - ALPHA, ALU.is_gt, ALU.mult))
            link(v.tensor_scalar(deg[:, 0:2, :], deg[:, 0:2, :], 1e-30, None, ALU.max))
            dve.sem_inc(root_in, 1)
            dve.wait_ge(root_done, 1)
            r2, t2, d2 = deg_t[:, 0:2, :], stat[:, :, :], deg[:, 0:2, :]
            link(v.reciprocal(r2, r2))
            link(v.tensor_tensor(t2, r2, r2, ALU.mult))
            link(v.tensor_tensor(t2, t2, d2, ALU.mult))
            link(v.tensor_scalar(t2, t2, -0.5, 1.5, ALU.mult, ALU.add))
            link(v.tensor_tensor(r2, r2, t2, ALU.mult))
            v.tensor_tensor(inv_out[:, :], inv_out[:, :], deg_t[:, 0, :], ALU.mult)
            v.tensor_tensor(inv_in9[:, :], inv_in9[:, :], deg_t[:, 1, :], ALU.mult)
            link(v.tensor_tensor_scan(deg[:, 2, :], ones[:, :], count[:, :], 0.0, ALU.mult, ALU.add))
            link(v.tensor_copy(first[:, :], deg[:, 2, NJ - 1:NJ]))
            dve.sem_inc(totals_ready, 1)
            dve.wait_ge(offsets_ready, 1)
            link(v.tensor_copy(first[:, :], proj[:, 0, 0:1]))
            link(v.tensor_scalar(deg[:, 2, :], deg[:, 2, :], first[:, 0:1], float(-1 - ZERO_ROW), ALU.add, ALU.add))
            link(v.tensor_scalar(deg_t[:, 2, :], count[:, :], 0.0, None, ALU.is_gt))
            link(v.tensor_tensor(deg[:, 2, :], deg[:, 2, :], deg_t[:, 2, :], ALU.mult))
            link(v.tensor_scalar(end_idx[:, 0:NJ], deg[:, 2, :], float(ZERO_ROW), None, ALU.add))
            link(v.tensor_copy(end_idx[:, NJ:NJ + 2 * NB], end_idx[:, 0:2 * NB]))
            dve.wait_ge(loaded_x, 48)
            link(v.tensor_tensor(u_sb[:, :].rearrange("p (j f) -> p j f", f=D), x_sb[:, :].rearrange("p (j f) -> p j f", f=D),
                                 inv_out[:, :].unsqueeze(2).broadcast_to([P, NJ, D]), ALU.mult))
            dve.sem_inc(node_init, 1)

            def stage(b, at):
                v.tensor_copy(src_st[:, b, :], src_idx[:, at])
                v.tensor_copy(dst_st[:, b, :], dst_idx[:, at])
                v.tensor_copy(w_st[:, b, :], w_p[:, at]).then_inc(staged, 1)

            for b in range(2):
                stage(b, bass.ds(b * CT, CT))
                v.tensor_copy(end_st[:, b, :], end_idx[:, b * NB:(b + 1) * NB]).then_inc(end_staged, 1)

            def scan(q, b, g):
                G = (q * 2 + b) * CG + g
                dve.wait_ge(fwd_done, G + 1 + FREE_G)
                dve.wait_ge(back_done, G + 1)
                if g == 0:
                    dve.wait_ge(same_ready[b], (q + 1) * 16)
                    before = sums[0:D, 1 - b, CE - 1:CE]
                else:
                    before = sums[0:D, b, g * GE - 1:g * GE]
                dve.wait_ge(scan_done, G + FREE_F)
                v.tensor_tensor_scan(sums[0:D, b, g * GE:(g + 1) * GE], same[:, b, g * GE:(g + 1) * GE],
                                     bank(b, g), before, ALU.mult, ALU.add).then_inc(scan_done, 1)

            bank = lambda b, g: fwd[0:D, g, :]
            for part in range(PARTS):
                with dve.Fori(0, PART_STEPS) as kk:
                    k = kk + part * PART_STEPS
                    with dve.Fori(0, PAIRS) as i:
                        for b in range(2):
                            for g in range(CG):
                                scan(k * PAIRS + i, b, g)
                            stage(b, bass.ds(i * (2 * CT) + (b + 2) * CT, CT))
                    with dve.Fori(0, NODE_PAIRS) as j:
                        for b in range(2):
                            blk = k * NODE_PAIRS + j
                            step = Chain(dve, vec_node, (blk * 2 + b) * 4)
                            dve.wait_ge(ends_gathered[b], (blk + 1) * (16 * NB))
                            cols = bass.ds((j * 2 + b) * (NB * D), NB * D)
                            nodes = bass.ds((j * 2 + b) * NB, NB)
                            u3 = u_sb[:, cols].rearrange("p (j f) -> p j f", f=D)
                            h3 = h_sb[:, cols].rearrange("p (j f) -> p j f", f=D)
                            e3 = ends_in[:, b, :, :]
                            step(v.tensor_tensor(e3, e3, u3, ALU.add))
                            step(v.tensor_tensor(e3, e3, inv_in9[:, nodes].unsqueeze(2).broadcast_to([P, NB, D]), ALU.mult))
                            step(v.scalar_tensor_tensor(h_sb[:, cols], x_sb[:, cols], ALPHA, e3.rearrange("p j f -> p (j f)"), ALU.mult, ALU.add))
                            step(v.tensor_tensor(u3, h3, inv_out[:, nodes].unsqueeze(2).broadcast_to([P, NB, D]), ALU.mult))
                            v.tensor_copy(end_st[:, b, :], end_idx[:, bass.ds((j * 2 + b + 2) * NB, NB)]).then_inc(end_staged, 1)
                            dve.sem_inc(node_done, 1)

            norm = Chain(dve, vec_ln)

            def layernorm(o, s, t, nth):
                s3, t3, o3 = (z[:, :].rearrange("p (j f) -> p j f", f=D) for z in (s, t, o))
                norm(v.tensor_reduce(stat[:, 0, :], s3, AX, ALU.add))
                norm(v.tensor_scalar(stat[:, 0, :], stat[:, 0, :], 1.0 / D, None, ALU.mult))
                norm(v.tensor_tensor(s3, s3, stat[:, 0, :].unsqueeze(2).broadcast_to([P, NJ, D]), ALU.subtract))
                norm(v.tensor_tensor(t3, s3, s3, ALU.mult))
                norm(v.tensor_reduce(stat[:, 1, :], t3, AX, ALU.add))
                norm(v.tensor_scalar(stat[:, 1, :], stat[:, 1, :], 1.0 / D, EPS, ALU.mult, ALU.add))
                dve.sem_inc(root_in, 1)
                dve.wait_ge(root_done, nth)
                norm(v.reciprocal(stat[:, 1, :], stat[:, 0, :]))
                norm(v.tensor_tensor(o3, s3, stat[:, 1, :].unsqueeze(2).broadcast_to([P, NJ, D]), ALU.mult))

            dve.wait_ge(node_stored, (STEPS + 1) * (16 * NODE_BLOCKS))
            norm(v.tensor_tensor(h_sb[:, :], h_sb[:, :], x_sb[:, :], ALU.add))
            layernorm(x_sb, h_sb, tmp, 2)
            v.memset(u_sb[D:D + 1, :], 1.0).then_inc(ones_row, 1)

            with dve.Fori(0, NODE_PAIRS) as j:
                for b in range(2):
                    n = j * 2 + b
                    v.tensor_copy(x_st[:, b, :, :].rearrange("p j f -> p (j f)"), x_sb[:, bass.ds(n * (NB * D), NB * D)]).then_inc(x1_staged, 1)
                    dve.wait_ge(kvq_done, n + 1 + 2)
                    f2 = fwd[:, :, 0:2 * 3 * D].rearrange("p a (j f) -> p a j f", f=3 * D)
                    o2 = kvq_out[:, b, 0:NB - 1, :].rearrange("p (a j) f -> p a j f", j=2)
                    v.tensor_copy(o2, f2[:, 0:3])
                    v.tensor_copy(kvq_out[:, b, NB - 1, :], f2[:, 3, 0, :]).then_inc(kvq_copied, 1)
                for b in range(2):
                    dve.wait_ge(kvq_stored[b], (j + 1) * 32)

            for b in range(2):
                dve.wait_ge(kvq_stored[b], 32 * NODE_PAIRS)
            isd = float(1.0 / float(DH) ** 0.5)
            bank = lambda b, g: fwd[0:D, 2 + g % 2, :]
            EC = 6
            with dve.Fori(0, PAIRS) as i:
                q = i + STEPS * PAIRS
                for b in range(2):
                    dve.wait_ge(gathered[PARTS][b], (i + 1) * (32 * CT))
                    for g in range(CG):
                        Gl = (i * 2 + b) * CG + g
                        edge = Chain(dve, vec_edge, Gl * EC)
                        t0, t1 = g * GT, (g + 1) * GT
                        k4, v4, q4 = kv_in[:, b, t0:t1, 0:D], kv_in[:, b, t0:t1, D:2 * D], rows_in[:, b, t0:t1, :]
                        s4 = score[:, g % 2, :, :]
                        p4 = prod[:, g % 2, :, :]
                        edge(v.tensor_tensor(p4, k4, q4, ALU.mult))
                        dve.wait_ge(eproj_done, Gl + 1 + 2)
                        edge(v.tensor_tensor(p4, p4, proj[:, g % 2, 0:GT * D].rearrange("p (t f) -> p t f", f=D), ALU.mult))
                        edge(v.tensor_reduce(s4, p4.rearrange("p t (h d) -> p t h d", d=DH), AX, ALU.add))
                        edge(v.tensor_scalar(s4, s4, isd, 5.0, ALU.mult, ALU.min))
                        edge(v.tensor_scalar(s4, s4, -5.0, None, ALU.max))
                        dve.sem_inc(clipped, 1)
                        dve.wait_ge(exp_done, Gl + 1)
                        dve.wait_ge(fwd_done, Gl + STEPS * NCH * CG + FREE_G - 3)
                        edge(v.tensor_tensor(msg[:, g, :, :].rearrange("p t (h d) -> p t h d", d=DH), v4.rearrange("p t (h d) -> p t h d", d=DH),
                                             s4.unsqueeze(3).broadcast_to([P, GT, HEADS, DH]), ALU.mult))
                        dve.sem_inc(kv_used, 1)
                        scan(q, b, g)
                    stage(b, bass.ds(i * (2 * CT) + (b + 2) * CT, CT))
            with dve.Fori(0, NODE_PAIRS) as j:
                for b in range(2):
                    blk = j + STEPS * NODE_PAIRS
                    dve.wait_ge(ends_gathered[b], (blk + 1) * (16 * NB))
                    cols = bass.ds((j * 2 + b) * (NB * D), NB * D)
                    v.tensor_tensor(h_sb[:, cols], ends_in[:, b, :, :].rearrange("p j f -> p (j f)"), x_sb[:, cols], ALU.add).then_inc(node_done, 1)
                    v.tensor_copy(end_st[:, b, :], end_idx[:, bass.ds((j * 2 + b + 2) * NB, NB)]).then_inc(end_staged, 1)
            dve.wait_ge(node_done, 2 + (STEPS + 1) * NODE_BLOCKS)
            layernorm(h_sb, h_sb, tmp, 3)
            dve.sem_inc(y_done, 1)

        @block.tensor
        def _(pe):
            pe.sem_inc(fwd_done, FREE_G)
            pe.sem_inc(back_done, FREE_G)
            pe.sem_inc(hots_used, 2)
            pe.sem_inc(attrT_done, 2)
            pe.sem_inc(eproj_done, 2)
            pe.sem_inc(kvq_done, 2)
            pe.sem_inc(kv_used, FREE_G)
            pe.wait_ge(consts, 3)
            pe.wait_ge(nat_ready, 1)
            n = 0
            for nat in (src_f, dst_f, w_nat):
                for r in range(QB):
                    rows = min(P, NQ - r * P)
                    if n >= 4:
                        pe.wait_ge(nat_T_used, n - 3)
                    for u in range(GT):
                        last = nc.tensor.transpose(fwd[:, n % 4, u * P:u * P + rows], nat[0:rows, r, u::GT], ident[0:rows, 0:rows])
                    last.then_inc(nat_T, 1)
                    n += 1
            nc.tensor.matmul(back[:, 0, 0:2 * NJ], zeros[:, 0:P], zeros[:, 0:2 * NJ], start=True, stop=False)
            nc.tensor.matmul(back[:, 1, 0:NJ], zeros[:, 0:P], zeros[:, 0:NJ], start=True, stop=False)
            with pe.Fori(0, NT_TILES // (2 * HB)) as i:
                for b in range(2):
                    wait_count(pe, hots_ready, i * 2 + b + 1)
                    for t in range(HB):
                        o = hots[:, b, t, :]
                        nc.tensor.matmul(back[:, 0, 0:2 * NJ], o[:, 0:P], o[:, P:P + 2 * NJ], start=False, stop=False)
                        last = nc.tensor.matmul(back[:, 1, 0:NJ], o[:, P + 2 * NJ:2 * P + 2 * NJ], o[:, 2 * P + 2 * NJ:HOT], start=False, stop=False)
                    last.then_inc(hots_used, 1)
            nc.tensor.matmul(back[:, 0, 0:2 * NJ], zeros[:, 0:P], zeros[:, 0:2 * NJ], start=False, stop=True)
            nc.tensor.matmul(back[:, 1, 0:NJ], zeros[:, 0:P], zeros[:, 0:NJ], start=False, stop=True).then_inc(counted, 1)
            pe.wait_ge(totals_ready, 1)
            nc.tensor.matmul(proj[:, 0, 0:1], lower[:, :], first[:, 0:1], start=True, stop=True).then_inc(offsets_ready, 1)

            def turn_back(q, b, g):
                G = (q * 2 + b) * CG + g
                wait_count(pe, scan_done, G + 1 + FREE_F)
                wait_count(pe, out_copied, G + 1)
                for u in range(GT):
                    last = nc.tensor.transpose(back[:, g % 2, u * D:(u + 1) * D], sums[0:D, b, g * GE + u:(g + 1) * GE:GT], ident[0:D, 0:D])
                last.then_inc(back_done, 1)

            for part in range(PARTS):
                with pe.Fori(0, PART_STEPS) as kk:
                    k = kk + part * PART_STEPS
                    with pe.Fori(0, PAIRS) as i:
                        q = k * PAIRS + i
                        for b in range(2):
                            for g in range(CG):
                                G = (q * 2 + b) * CG + g
                                wait_count(pe, scaled_done, G + 1 + FREE_G)
                                wait_count(pe, scan_done, G + 1)
                                for u in range(GT):
                                    last = nc.tensor.transpose(fwd[0:D, g, u::GT], scaled[:, b, g * GT + u, :], ident[:, :])
                                last.then_inc(fwd_done, 1)
                                if g > 0:
                                    turn_back(q, b, g - 1)
                            turn_back(q, b, CG - 1)

            pe.wait_ge(loaded_w, 16 * 8)
            pe.wait_ge(ones_row, 1)
            with pe.Fori(0, NODE_PAIRS) as j:
                for b in range(2):
                    n = j * 2 + b
                    wait_count(pe, x1_staged, n + 1)
                    for t in range(NB):
                        last = nc.tensor.transpose(proj[0:D, t // 4, (t % 4) * P:(t % 4 + 1) * P], x_st[:, b, t, :], ident[:, :])
                    last.then_inc(x1T_done, 1)
                    wait_count(pe, x1T_copied, n + 1)
                    for t in range(NB):
                        last = nc.tensor.matmul(fwd[:, t // 2, (t % 2) * 3 * D:(t % 2 + 1) * 3 * D], xT[:, b, t, :], w_kvq[:, :], start=True, stop=True)
                    last.then_inc(kvq_done, 1)
                    wait_count(pe, kvq_copied, n + 1)

            def attr(G, g):
                b = g // CG
                if g % CG == 0:
                    wait_count(pe, attr_loaded[b], (i + 1) * 16)
                for u in range(GT):
                    last = nc.tensor.transpose(fwd[0:D, g % 2, u * P:(u + 1) * P], attr_in[:, b, (g % CG) * GT + u, :], ident[:, :])
                last.then_inc(attrT_done, 1)
                wait_count(pe, attrT_copied, G + 1)
                for u in range(GT):
                    last = nc.tensor.matmul(proj[:, g % 2, u * D:(u + 1) * D], attrT[:, g % 2, u * P:(u + 1) * P], w_e[:, :], start=True, stop=True)
                last.then_inc(eproj_done, 1)

            with pe.Fori(0, PAIRS) as i:
                q = i + STEPS * PAIRS
                attr(i * (2 * CG), 0)
                for g in range(2 * CG):
                    Gl = i * (2 * CG) + g
                    if g + 1 < 2 * CG:
                        attr(Gl + 1, g + 1)
                    wait_count(pe, kv_used, Gl + 1 + FREE_G)
                    for u in range(GT):
                        last = nc.tensor.transpose(fwd[0:D, 2 + g % 2, u::GT], msg[:, g % CG, u, :], ident[:, :])
                    last.then_inc(fwd_done, 1)
                    turn_back(q, g // CG, g % CG)


_INS = ['x', 'src', 'dst', 'edge_attr_64', 'edge_weight', 'L1_gnn_WQ', 'L1_gnn_bQ', 'L1_gnn_WK', 'L1_gnn_bK',
        'L1_gnn_WE', 'L1_gnn_bE', 'L1_gnn_WV', 'L1_gnn_bV']
_OUTS = [((12500, 64), 'float32')]


def kernel(**inputs):
    import numpy as _np
    import concourse.bacc as _bacc
    from concourse import mybir as _mybir
    from concourse.bass_utils import run_bass_kernel_spmd as _run

    nc = _bacc.Bacc("TRN2", target_bir_lowering=False, num_devices=1)
    arrays, args = {}, []
    for name in _INS:
        a = _np.ascontiguousarray(inputs[name])
        arrays[f"in_{name}_dram"] = a
        args.append(nc.dram_tensor(f"in_{name}_dram", a.shape, _mybir.dt.from_np(a.dtype), kind="ExternalInput").ap())
    for i, (shape, dtype) in enumerate(_OUTS):
        dt = _mybir.dt.from_np(_np.dtype(dtype))
        args.append(nc.dram_tensor(f"out_{i}_dram", shape, dt, kind="ExternalOutput").ap())
    build(nc, *args)
    r = _run(nc, [arrays], core_ids=[0])
    got = tuple(r.results[0][f"out_{i}_dram"] for i in range(len(_OUTS)))
    return got[0]
```

```python
from contextlib import ExitStack

import concourse.bass as bass
from concourse import mybir

F32 = mybir.dt.float32
BF16 = mybir.dt.bfloat16
I32 = mybir.dt.int32
U32 = mybir.dt.uint32
ALU = mybir.AluOpType
ACT = mybir.ActivationFunctionType
AX = mybir.AxisListType.X

P = 128
STEPS = 10
ALPHA = 0.1
EPS = 1e-5
HEADS = 8
GT = 4
GE = GT * P
CG = 4
CT = CG * GT
CE = CG * GE
NB = 10
POS_DENSE = 27
NODE_DENSE = 40
DENSE_PITCH = 4096
ROUND = 12582912.0


class Chain:

    def __init__(self, eng, sem, base=0):
        self.eng, self.sem, self.base, self.n = eng, sem, base, 0

    def __call__(self, ins):
        self.n += 1
        ins.then_inc(self.sem, 1)
        self.eng.wait_ge(self.sem, self.base + self.n)


def build(nc, x, src, dst, edge_attr, edge_weight, WQ, bQ, WK, bK, WE, bE, WV, bV, out):
    N, D = x.shape
    E = src.shape[0]
    DH = D // HEADS
    NJ = -(-N // P // (2 * NB)) * 2 * NB
    NP = N // NJ
    assert NP * NJ == N and NP <= P
    assert NJ % (2 * NB) == 0 and D == 64 and DH * HEADS == D
    NT = P * NJ
    NCH = -(-E // CE)
    assert NCH % 2 == 0
    PAIRS = NCH // 2
    EP = NCH * CE
    NQ = EP // GE
    QB = -(-NQ // P)
    NT_TILES = NQ * GT
    WRAP = 2 * CG
    NODE_PAIRS = NJ // (2 * NB)
    NODE_BLOCKS = 2 * NODE_PAIRS
    F_PAIR = POS_DENSE
    DE = F_PAIR * 2 * CE
    DN = NODE_DENSE * NJ
    DQ = DE // GE
    DT = DE // P
    DH8 = DT // 8
    UNIT_J = 5
    D_ITERS = NJ // UNIT_J
    DC = DN // 8
    SLOTS = 5
    assert DC <= 512 and DN % 8 == 0 and D_ITERS < PAIRS - F_PAIR and DT % 16 == 0 and DE < E and DN < DENSE_PITCH - 1
    FAST_PARTS = [(0, STEPS - 1), (STEPS - 1, 1)]
    ALL_PARTS = [(0, 5), (5, STEPS - 6), (STEPS - 1, 1)]
    for first_pair, parts in ((F_PAIR, FAST_PARTS), (0, ALL_PARTS)):
        assert all(n * (PAIRS - first_pair) * 16 * CT < 65536 for _, n in parts)
    ZERO_ROW = EP
    QF = E // GE
    REST = E - QF * GE

    node_rows = nc.dram_tensor("node_rows", [NT, D], F32).ap()
    edge_rows = nc.dram_tensor("edge_rows", [EP + P, D], F32).ap()
    late_rows = nc.dram_tensor("late_rows", [EP - DE + P, D], F32).ap()
    same_rows = nc.dram_tensor("same_rows", [(NQ + WRAP) * GE], BF16).ap()
    dense = nc.dram_tensor("dense", [P * NJ * DENSE_PITCH, 1], F32).ap()
    dense_rows = nc.dram_tensor("dense_rows", [DN, D], F32).ap()
    attr_rows = nc.dram_tensor("attr_rows", [EP, D], F32).ap()
    kv_rows = nc.dram_tensor("kv_rows", [NT, 2 * D], F32).ap()
    q_rows = nc.dram_tensor("q_rows", [NT, D], F32).ap()

    dense_v = dense.rearrange("(p j c) o -> p j (c o)", j=NJ, c=DENSE_PITCH)
    node_rows_v = node_rows.rearrange("(p j) f -> p (j f)", j=NJ)
    kv_rows_v = kv_rows.rearrange("(p j) f -> p j f", j=NJ)
    q_rows_v = q_rows.rearrange("(p j) f -> p j f", j=NJ)

    def sum_rows(F):
        return late_rows if F else edge_rows

    def by_group(rows):
        return rows[0:rows.shape[0] - P, :].rearrange("(g p u) f -> p g (u f)", p=P, u=GT)

    attr_rows_v = attr_rows.rearrange("(g p u) f -> p g (u f)", p=P, u=GT)

    with ExitStack() as ctx:
        def sb(name, shape, dt=F32):
            return ctx.enter_context(nc.sbuf_tensor(name, shape, dt))

        def sem(name):
            return ctx.enter_context(nc.semaphore(name))

        x_sb = sb("x_sb", [P, NJ * D])
        u_sb = sb("u_sb", [P, NJ * D])
        big = sb("big", [P, 2 * NJ * D])
        h_sb, tmp = big[:, 0:NJ * D], big[:, NJ * D:2 * NJ * D]
        ring = big[:, 0:SLOTS * 4 * DC].rearrange("p (s t c) -> p s t c", s=SLOTS, t=2)
        dense_sum = big[:, SLOTS * 4 * DC:SLOTS * 4 * DC + 4 * DC]
        dense_out = big[:, 0:NODE_DENSE * D].rearrange("p (a t f) -> p a t f", t=2, f=D)
        dense_n = big[:, NODE_DENSE * D:NODE_DENSE * D + NJ * D]
        src_idx = sb("src_idx", [P, (NQ + WRAP) * GT], I32)
        dst_idx = sb("dst_idx", [P, (NQ + WRAP) * GT], I32)
        w_p = sb("w_p", [P, (NQ + WRAP) * GT])
        end_idx = sb("end_idx", [P, NJ + 2 * NB], I32)
        rows_in = sb("rows_in", [P, 2, CT, D])
        scaled = sb("scaled", [P, 2, CT, D])
        sums = sb("sums", [P, 2, CE])
        same = sb("same", [D, 2, CE], BF16)
        rows_out = sb("rows_out", [P, 2, CT, D])
        u_st = sb("u_st", [P, UNIT_J * D])
        dense_idx = sb("dense_idx", [P, DT], I32)
        add_idx = sb("add_idx", [P, 2, 8], I32)
        add_w = sb("add_w", [P, 2, 8])
        repeats = sb("repeats", [P, 8])
        all_ends = sb("all_ends", [P, NJ], I32)
        flag = sb("flag", [1, 1], I32)
        bad = sb("bad", [P, 2])
        earlier = sb("earlier", [P, P])
        src_st = sb("src_st", [P, 2, CT], I32)
        dst_st = sb("dst_st", [P, 2, CT], I32)
        w_st = sb("w_st", [P, 2, CT])
        end_st = sb("end_st", [P, 2, NB], I32)
        ends_in = sb("ends_in", [P, 2, NB, D])
        ident = sb("ident", [P, P])
        lower = sb("lower", [P, P])
        iota_p = sb("iota_p", [P, P])
        iota_j = sb("iota_j", [P, NJ])
        ones = sb("ones", [P, NJ])
        zeros = sb("zeros", [P, 512])
        inv_out = sb("inv_out", [P, NJ])
        inv_in9 = sb("inv_in9", [P, NJ])
        deg = sb("deg", [P, 3, NJ])
        deg_t = sb("deg_t", [P, 3, NJ])
        count = sb("count", [P, NJ])
        first = sb("first", [P, 1])
        w_kvq = sb("w_kvq", [D + 1, 3 * D])
        w_e = sb("w_e", [D + 1, D])
        stat = sb("stat", [P, 2, NJ])
        score = sb("score", [P, 2, GT, HEADS])

        nat_i = tmp[:, 0:3 * QB * GE].rearrange("p (a r i) -> p a r i", a=3, i=GE)
        src_nat, dst_nat = nat_i[:, 0].bitcast(I32), nat_i[:, 1].bitcast(I32)
        w_nat = nat_i[:, 2]
        nat_f = u_sb[:, 0:3 * QB * GE].rearrange("p (a r i) -> p a r i", a=3, i=GE)
        prev_nat, dst_f, prev_f = nat_f[:, 0].bitcast(I32), nat_f[:, 1], nat_f[:, 2]
        src_f = sums[:, :, :].rearrange("p a e -> p (a e)")[:, 0:QB * GE].rearrange("p (r i) -> p r i", i=GE)
        same_nat = x_sb[:, 0:QB * GE // 2].bitcast(BF16).rearrange("p (r i) -> p r i", i=GE)
        src_nf = h_sb[:, 0:QB * GE].rearrange("p (r i) -> p r i", i=GE)
        src_pf = rows_in[:, :, :, :].rearrange("p a t f -> p (a t f)")[:, 0:NT_TILES]
        dst_pf = scaled[:, :, :, :].rearrange("p a t f -> p (a t f)")[:, 0:NT_TILES]
        digits = tmp[:, 0:4 * NT_TILES].rearrange("p (a t) -> p a t", a=4)
        src_hi, src_lo, dst_hi, dst_lo = (digits[:, a] for a in range(4))
        blank = rows_out[:, :, :, :].rearrange("p b t f -> p (b t f)")
        row_in = u_sb[:, 0:6 * 8 * P].rearrange("p (b a e) -> p b a e", b=2, a=3)
        eq_src = sums[:, 0, 0:8 * P].rearrange("p (t e) -> p t e", e=P)
        eq_both = sums[:, 0, 8 * P:16 * P].rearrange("p (t e) -> p t e", e=P)
        HOT = 2 * P + 3 * NJ
        HB = 4
        hots = h_sb[:, 0:2 * HB * HOT].rearrange("p (b t c) -> p b t c", b=2, c=HOT)
        eq_junk = h_sb[:, 2 * HB * HOT:2 * HB * HOT + 8 * P].rearrange("p (t e) -> p t e", e=P)

        kvq_out = tmp[:, 0:2 * NB * 3 * D].rearrange("p (b j f) -> p b j f", b=2, f=3 * D)
        x_st = tmp[:, 2 * NB * 3 * D:2 * NB * 4 * D].rearrange("p (b j f) -> p b j f", b=2, f=D)
        xT = u_sb[0:D + 1, 0:2 * NB * P].rearrange("p (b j n) -> p b j n", b=2, n=P)
        kv_in = u_sb[:, 0:2 * CT * 2 * D].rearrange("p (b t f) -> p b t f", b=2, f=2 * D)
        attrT = u_sb[0:D + 1, 2 * CT * 2 * D:2 * CT * 2 * D + 2 * GE].rearrange("p (b e) -> p b e", b=2)
        attr_in = tmp[:, 0:2 * CT * D].rearrange("p (b t f) -> p b t f", b=2, f=D)
        prod = tmp[:, 2 * CT * D:2 * CT * D + 2 * GT * D].rearrange("p (b t f) -> p b t f", b=2, f=D)
        msg = tmp[:, 2 * CT * D + 2 * GT * D:2 * CT * D + 6 * GT * D].rearrange("p (b t f) -> p b t f", b=4, f=D)

        x1_ps_all = ctx.enter_context(nc.psum_tensor("banks", [P, 8, GE], F32))
        fwd, back, proj = x1_ps_all[:, 0:4, :], x1_ps_all[:, 4:6, :], x1_ps_all[:, 6:8, :]

        x1T_ps = x1_ps_all[:, 5:8, :].rearrange("p b e -> p (b e)")

        def kvq_ps(r):
            return x1_ps_all[:, r, :]

        loaded_e = sem("loaded_e")
        loaded_x = sem("loaded_x")
        loaded_w = sem("loaded_w")
        attr_copied = sem("attr_copied")
        cleared = sem("cleared")
        consts = sem("consts")
        vec_pre = sem("vec_pre")
        vec_node = sem("vec_node")
        vec_ln = sem("vec_ln")
        vec_edge = sem("vec_edge")
        nat_ready = sem("nat_ready")
        same_nat_ready = sem("same_nat_ready")
        same_stored = sem("same_stored")
        nat_T = sem("nat_T")
        nat_T_used = sem("nat_T_used")
        hots_ready = sem("hots_ready")
        hots_used = sem("hots_used")
        counted = sem("counted")
        root_in = sem("root_in")
        root_done = sem("root_done")
        totals_ready = sem("totals_ready")
        offsets_ready = sem("offsets_ready")
        node_init = sem("node_init")
        dense_cleared = sem("dense_cleared")
        nat_T_all = sem("nat_T_all")
        row_loaded = [sem("row_loaded0"), sem("row_loaded1")]
        row_used = sem("row_used")
        add_ready = sem("add_ready")
        add_used = sem("add_used")
        added = sem("added")
        vec_add = sem("vec_add")
        bad_ready = sem("bad_ready")
        bad_summed = sem("bad_summed")
        flag_ready = sem("flag_ready")

        class EdgeSems:

            def __init__(self, name, parts, slots=0):
                def one(what):
                    return sem(f"{what}_{name}")

                def pair(what):
                    return [sem(f"{what}_{name}{b}") for b in range(2)]

                self.staged = one("staged")
                self.gathered = [pair(f"gathered{part}") for part in range(parts)]
                self.scaled_done = one("scaled_done")
                self.fwd_done = one("fwd_done")
                self.same_ready = pair("same_ready")
                self.scan_done = one("scan_done")
                self.back_done = one("back_done")
                self.out_copied = one("out_copied")
                self.rows_stored = pair("rows_stored")
                self.end_staged = one("end_staged")
                self.ends_gathered = pair("ends_gathered")
                self.node_done = one("node_done")
                self.node_stored = one("node_stored")
                self.vec_first = one("vec_first")
                self.vec_node = one("vec_node")
                self.restarted = one("restarted")
                if slots:
                    self.ring_ready = [sem(f"ring_ready_{name}{n}") for n in range(slots)]
                    self.u_staged = one("u_staged")
                    self.dense_done = one("dense_done")
                    self.acc_done = one("acc_done")
                    self.sum_copied = one("sum_copied")
                    self.turned = one("turned")
                    self.out_turned = one("out_turned")
                    self.dense_stored = one("dense_stored")
                    self.dense_loaded = one("dense_loaded")

        S_DENSE = EdgeSems("dense", len(FAST_PARTS), SLOTS)
        S_ALL = EdgeSems("all", len(ALL_PARTS))
        S_ATT = EdgeSems("att", 1)
        x1_staged = sem("x1_staged")
        x1T_done = sem("x1T_done")
        x1T_copied = sem("x1T_copied")
        kvq_done = sem("kvq_done")
        kvq_copied = sem("kvq_copied")
        kvq_stored = [sem("kvq_stored0"), sem("kvq_stored1")]
        ones_row = sem("ones_row")
        attr_loaded = [sem("attr_loaded0"), sem("attr_loaded1")]
        attrT_done = sem("attrT_done")
        attrT_copied = sem("attrT_copied")
        eproj_done = sem("eproj_done")
        clipped = sem("clipped")
        exp_done = sem("exp_done")
        kv_used = sem("kv_used")
        y_done = sem("y_done")
        y_stored = sem("y_stored")
        blank_ready = sem("blank_ready")
        passed = sem("passed")

        def wait_count(eng, sem, count):
            eng.wait_ge(sem, count)
            eng.sem_inc(passed, 1)

        FREE_G = 2 * CG
        FREE_F = 2
        FREE_R = SLOTS
        FREE_B = 2

        block = ctx.enter_context(nc.Block())

        def choose(eng):
            way = eng.alloc_register(f"way_{eng.engine.name}")
            eng.wait_ge(flag_ready, 1)
            eng.reg_load(way, flag[0:1, 0:1])
            return way

        @block.sync
        def _(sp):
            sp.wait_ge(cleared, 1)
            for a, nat in ((src, src_nat), (dst, dst_nat), (edge_weight, w_nat)):
                full = (QB - 1) * P
                sp.dma_start(nat[:, 0:QB - 1, :], a[0:full * GE].rearrange("(r p i) -> p r i", p=P, i=GE)).then_inc(loaded_e, 16)
                sp.dma_start(nat[0:QF - full, QB - 1, :], a[full * GE:QF * GE].rearrange("(p i) -> p i", i=GE)).then_inc(loaded_e, 16)
                sp.dma_start(nat[QF - full:QF - full + 1, QB - 1, 0:REST], a[QF * GE:E].rearrange("(p i) -> p i", p=1)).then_inc(loaded_e, 16)
            full = (QB - 1) * P
            sp.dma_start(prev_nat[0:1, 0, 1:GE], dst[0:GE - 1].rearrange("(p i) -> p i", p=1)).then_inc(loaded_e, 16)
            sp.dma_start(prev_nat[1:P, 0, :], dst[GE - 1:P * GE - 1].rearrange("(p i) -> p i", i=GE)).then_inc(loaded_e, 16)
            sp.dma_start(prev_nat[:, 1:QB - 1, :], dst[P * GE - 1:full * GE - 1].rearrange("(r p i) -> p r i", p=P, i=GE)).then_inc(loaded_e, 16)
            sp.dma_start(prev_nat[0:QF - full, QB - 1, :], dst[full * GE - 1:QF * GE - 1].rearrange("(p i) -> p i", i=GE)).then_inc(loaded_e, 16)
            sp.dma_start(prev_nat[QF - full:QF - full + 1, QB - 1, 0:REST], dst[QF * GE - 1:E - 1].rearrange("(p i) -> p i", p=1)).then_inc(loaded_e, 16)
            sp.dma_start(w_kvq[0:D, 0:D], WK).then_inc(loaded_w, 16)
            sp.dma_start(w_kvq[0:D, D:2 * D], WV).then_inc(loaded_w, 16)
            sp.dma_start(w_kvq[0:D, 2 * D:3 * D], WQ).then_inc(loaded_w, 16)
            sp.dma_start(w_e[0:D, :], WE).then_inc(loaded_w, 16)
            for b, to in ((bK, w_kvq[D:D + 1, 0:D]), (bV, w_kvq[D:D + 1, D:2 * D]), (bQ, w_kvq[D:D + 1, 2 * D:3 * D]), (bE, w_e[D:D + 1, :])):
                sp.dma_start(to, b.rearrange("(p f) -> p f", p=1)).then_inc(loaded_w, 16)
            sp.wait_ge(blank_ready, 1)
            DZ = 20
            for j0 in range(0, NJ, DZ):
                sp.dma_start(dense_v[:, j0:j0 + DZ, :].rearrange("p j (s c) -> p (j s) c", s=2),
                             blank.unsqueeze(1).broadcast_to([P, 2 * DZ, DENSE_PITCH // 2])).then_inc(dense_cleared, 16)
            sp.wait_ge(same_nat_ready, 1)
            full = (QB - 1) * P
            sp.dma_start(same_rows[0:full * GE].rearrange("(r p i) -> p r i", p=P, i=GE), same_nat[:, 0:QB - 1, :]).then_inc(same_stored, 16)
            sp.dma_start(same_rows[full * GE:NQ * GE].rearrange("(p i) -> p i", i=GE), same_nat[0:NQ - full, QB - 1, :]).then_inc(same_stored, 16)
            sp.wait_ge(cleared, 2)
            for p0, p1 in ((0, 112), (112, NP)):
                sp.dma_start(x_sb[p0:p1, :], x[p0 * NJ:p1 * NJ, :].rearrange("(p j) f -> p (j f)", j=NJ)).then_inc(loaded_x, 16)
            sp.wait_ge(nat_T_all, 1)
            with sp.Fori(0, DH8 // 2) as i:
                for b in range(2):
                    sp.wait_ge(row_used, i * 2 + b + 1)
                    at = bass.ds(i * (16 * P) + b * 8 * P, 8 * P)
                    for a, of in enumerate((src, dst)):
                        sp.dma_start(row_in[:, b, a, :].bitcast(I32), of[at].partition_broadcast(P)).then_inc(row_loaded[b], 16)
                    sp.dma_start(row_in[:, b, 2, :], edge_weight[at].partition_broadcast(P)).then_inc(row_loaded[b], 16)

            def zero_ends(S, F):
                rows, half = sum_rows(F), P // 2
                end = rows.shape[0] - P
                for b in range(2):
                    sp.dma_start(rows[end + b * half:end + (b + 1) * half, :], zeros[0:half, 0:D]).then_inc(S.rows_stored[b], 16)

            def load_same(S, b, at):
                sp.dma_start(same[:, b, :], same_rows[at].partition_broadcast(D)).then_inc(S.same_ready[b], 16)

            def edge_chunk(S, F, q, i, b):
                c = q * 2 + b
                sp.wait_ge(S.scan_done, c * CG + CG + FREE_F)
                load_same(S, b, bass.ds(i * (2 * CE) + (2 * F + b + 2) * CE, CE))
                sp.wait_ge(S.out_copied, c * CG + CG + FREE_B)
                sp.dma_start(by_group(sum_rows(F))[:, bass.ds(i * (2 * CG) + b * CG, CG), :],
                             rows_out[:, b, :, :].rearrange("p (g u) f -> p g (u f)", u=GT)).then_inc(S.rows_stored[b], 16)

            def load_unit(S, k, i, n):
                half, jj = n // UNIT_J, n % UNIT_J
                sp.wait_ge(S.dense_done, (k * D_ITERS + i) * (2 * UNIT_J) + n + 1)
                col = dense_v[:, bass.ds(i * UNIT_J + jj, 1), 0:DN].rearrange("p j (t s c) -> p j t s c", t=2, s=2)[:, 0, :, half, :]
                sp.dma_start(ring[:, jj, :, :], col).then_inc(S.ring_ready[jj], 16)

            def first_marks(S, F):
                sp.dma_start(same_rows[NQ * GE:(NQ + WRAP) * GE].rearrange("(p i) -> p i", i=GE),
                             same_rows[F * 2 * CE:(F + 1) * 2 * CE].rearrange("(p i) -> p i", i=GE)).then_inc(S.restarted, 16)
                sp.wait_ge(S.restarted, 16)
                sp.dma_start(same_rows[NQ * GE:NQ * GE + 1].rearrange("(p i) -> p i", i=1), zeros[0:1, 0:1].bitcast(BF16)[:, 0:1]).then_inc(S.restarted, 16)
                sp.wait_ge(S.restarted, 32)
                for b in range(2):
                    load_same(S, b, slice((NQ + b * CG) * GE, (NQ + (b + 1) * CG) * GE))

            def store_steps(S, F, parts, dense_way):
                n_pairs = PAIRS - F
                first_marks(S, F)
                zero_ends(S, F)
                sp.wait_ge(node_init, 1)
                sp.dma_start(node_rows_v, u_sb[:, :]).then_inc(S.node_stored, 16)
                for k0, n_steps in parts:
                    with sp.Fori(0, n_steps) as kk:
                        k = kk + k0
                        if dense_way:
                            def pair(i, ahead):
                                for b in range(2):
                                    for n in range(UNIT_J):
                                        if b == 0:
                                            load_unit(S, k, i, UNIT_J + n)
                                        elif ahead:
                                            load_unit(S, k, i + 1, n)
                                    edge_chunk(S, F, k * n_pairs + i, i, b)
                            for n in range(UNIT_J):
                                load_unit(S, k, 0, n)
                            with sp.Fori(0, D_ITERS - 1) as i:
                                pair(i, True)
                            pair(D_ITERS - 1, False)
                            sp.wait_ge(S.out_turned, (k + 1) * 5 + 1)
                            for t in range(2):
                                sp.dma_start(dense_rows[t * DN // 2:(t + 1) * DN // 2, :].rearrange("(a j) f -> j a f", j=NJ),
                                             dense_out[0:NJ, :, t, :]).then_inc(S.dense_stored, 16)
                            sp.wait_ge(S.dense_stored, (k + 1) * 32)
                            sp.dma_start(dense_n[0:NODE_DENSE, :], dense_rows.rearrange("(p j) f -> p (j f)", j=NJ)).then_inc(S.dense_loaded, 16)
                            with sp.Fori(D_ITERS, n_pairs) as i:
                                for b in range(2):
                                    edge_chunk(S, F, k * n_pairs + i, i, b)
                        else:
                            with sp.Fori(0, n_pairs) as i:
                                for b in range(2):
                                    edge_chunk(S, F, k * n_pairs + i, i, b)
                        with sp.Fori(0, NODE_PAIRS) as j:
                            for b in range(2):
                                n = (k * NODE_PAIRS + j) * 2 + b
                                sp.wait_ge(S.node_done, n + 1 + 2)
                                cols = bass.ds((j * 2 + b) * (NB * D), NB * D)
                                sp.dma_start(node_rows_v[:, cols], u_sb[:, cols]).then_inc(S.node_stored, 16)
                for b in range(2):
                    sp.wait_ge(S.same_ready[b], 16 * (1 + STEPS * n_pairs))

            way = choose(sp)
            with sp.If_eq(way, 0):
                store_steps(S_DENSE, F_PAIR, FAST_PARTS, True)
            with sp.Else():
                store_steps(S_ALL, 0, ALL_PARTS, False)

            with sp.Fori(0, NODE_PAIRS) as j:
                for b in range(2):
                    n = j * 2 + b
                    sp.wait_ge(kvq_copied, n + 1)
                    sp.dma_start(kv_rows_v[:, bass.ds(n * NB, NB), :], kvq_out[:, b, :, 0:2 * D]).then_inc(kvq_stored[b], 16)
                    sp.dma_start(q_rows_v[:, bass.ds(n * NB, NB), :], kvq_out[:, b, :, 2 * D:3 * D]).then_inc(kvq_stored[b], 16)
            for b in range(2):
                sp.wait_ge(kvq_stored[b], 32 * NODE_PAIRS)
            sp.wait_ge(attr_copied, 16 * (2 + (EP - E) // 64))
            for b in range(2):
                load_same(S_ATT, b, slice(b * CE, (b + 1) * CE))
            zero_ends(S_ATT, 0)
            for b in range(2):
                sp.dma_start(attr_in[:, b, :, :].rearrange("p (g u) f -> p g (u f)", u=GT),
                             attr_rows_v[:, b * CG:(b + 1) * CG, :]).then_inc(attr_loaded[b], 16)

            def attr_load(i, b):
                sp.wait_ge(attrT_done, (i * 2 + b + 1) * CG + 2)
                sp.dma_start(attr_in[:, b, :, :].rearrange("p (g u) f -> p g (u f)", u=GT),
                             attr_rows_v[:, bass.ds(i * (2 * CG) + (b + 2) * CG, CG), :]).then_inc(attr_loaded[b], 16)

            with sp.Fori(0, PAIRS - 1) as i:
                for b in range(2):
                    attr_load(i, b)
                    edge_chunk(S_ATT, 0, i, i, b)
            for b in range(2):
                edge_chunk(S_ATT, 0, PAIRS - 1, PAIRS - 1, b)
            sp.wait_ge(y_done, 1)
            for p0, p1 in ((0, 112), (112, NP)):
                sp.dma_start(out[p0 * NJ:p1 * NJ, :].rearrange("(p j) f -> p (j f)", j=NJ), h_sb[p0:p1, :]).then_inc(y_stored, 16)
            sp.wait_ge(y_stored, 32)
            for b in range(2):
                sp.wait_ge(S_ATT.same_ready[b], 16 * (1 + PAIRS))

        @block.gpsimd
        def _(pool):
            g = nc.gpsimd
            pool.memset(zeros[:, :], 0.0).then_inc(consts, 1)
            pool.memset(ident[:, :], 0.0)
            pool.memset(lower[:, :], 1.0)
            pool.memset(earlier[:, :], 1.0)
            pool.iota(iota_p[:, :], pattern=[[1, P]], base=0, channel_multiplier=0, allow_small_or_imprecise_dtypes=True)
            pool.iota(iota_j[:, :], pattern=[[1, NJ]], base=0, channel_multiplier=0, allow_small_or_imprecise_dtypes=True)
            pool.memset(ones[:, :], 1.0).then_inc(consts, 1)
            pool.wait_ge(consts, 2)
            pool.affine_select(out=ident[:, :], in_=ident[:, :], compare_op=ALU.not_equal, fill=1.0, base=0,
                               pattern=[[-1, P]], channel_multiplier=1)
            pool.affine_select(out=lower[:, :], in_=lower[:, :], compare_op=ALU.is_gt, fill=0.0, base=0,
                               pattern=[[1, P]], channel_multiplier=-1)
            pool.affine_select(out=earlier[:, :], in_=earlier[:, :], compare_op=ALU.is_gt, fill=0.0, base=0,
                               pattern=[[-1, P]], channel_multiplier=1).then_inc(consts, 1)

            pool.wait_ge(dense_cleared, 16 * 5)
            with pool.Fori(0, DH8 // 2) as i:
                for b in range(2):
                    h = i * 2 + b
                    wait_count(pool, add_ready, h + 1)
                    for t in range(8):
                        g.indirect_dma_start(out=dense, out_offset=bass.IndirectOffsetOnAxis(ap=add_idx[:, b, t:t + 1].bitcast(U32), axis=0),
                                             in_=add_w[:, b, t:t + 1], in_offset=None, compute_op=ALU.add).then_inc(added, 16)
                        wait_count(pool, added, h * (8 * 16) + (t + 1) * 16)
                    pool.sem_inc(add_used, 1)

            def gather_ends(S, k, F):
                for b in range(2):
                    wait_count(pool, S.rows_stored[b], (k + 1) * (16 * (PAIRS - F)) + 16)
                with pool.Fori(0, NODE_PAIRS) as j:
                    for b in range(2):
                        n = (k * NODE_PAIRS + j) * 2 + b
                        wait_count(pool, S.end_staged, n + 1)
                        wait_count(pool, S.node_done, n + 1)
                        for t in range(NB):
                            g.indirect_dma_start(out=ends_in[:, b, t, :], out_offset=None, in_=sum_rows(F),
                                                 in_offset=bass.IndirectOffsetOnAxis(ap=end_st[:, b, t:t + 1].bitcast(U32), axis=0)).then_inc(S.ends_gathered[b], 16)

            def gather_steps(S, F, parts):
                n_pairs = PAIRS - F
                for part, (k0, n_steps) in enumerate(parts):
                    with pool.Fori(0, n_steps) as kk:
                        k = kk + k0
                        wait_count(pool, S.node_stored, k * (16 * NODE_BLOCKS) + 16)
                        with pool.Fori(0, n_pairs) as i:
                            for b in range(2):
                                c = (k * n_pairs + i) * 2 + b
                                wait_count(pool, S.staged, c + 1)
                                wait_count(pool, S.scaled_done, c * CG + CG)
                                for t in range(CT):
                                    g.indirect_dma_start(out=rows_in[:, b, t, :], out_offset=None, in_=node_rows,
                                                         in_offset=bass.IndirectOffsetOnAxis(ap=src_st[:, b, t:t + 1].bitcast(U32), axis=0)).then_inc(S.gathered[part][b], 16)
                        gather_ends(S, k, F)

            way = choose(pool)
            with pool.If_eq(way, 0):
                gather_steps(S_DENSE, F_PAIR, FAST_PARTS)
            with pool.Else():
                gather_steps(S_ALL, 0, ALL_PARTS)

            for b in range(2):
                pool.wait_ge(kvq_stored[b], 32 * NODE_PAIRS)
            with pool.Fori(0, PAIRS) as i:
                for b in range(2):
                    c = i * 2 + b
                    wait_count(pool, S_ATT.staged, c + 1)
                    wait_count(pool, kv_used, (c + 1) * CG)
                    for t in range(CT):
                        g.indirect_dma_start(out=kv_in[:, b, t, :], out_offset=None, in_=kv_rows,
                                             in_offset=bass.IndirectOffsetOnAxis(ap=src_st[:, b, t:t + 1].bitcast(U32), axis=0)).then_inc(S_ATT.gathered[0][b], 16)
                        g.indirect_dma_start(out=rows_in[:, b, t, :], out_offset=None, in_=q_rows,
                                             in_offset=bass.IndirectOffsetOnAxis(ap=dst_st[:, b, t:t + 1].bitcast(U32), axis=0)).then_inc(S_ATT.gathered[0][b], 16)
            gather_ends(S_ATT, 0, 0)

        @block.scalar
        def _(act):
            act.wait_ge(root_in, 1)
            nc.scalar.activation(deg_t[:, 0:2, :], deg[:, 0:2, :], ACT.Sqrt).then_inc(root_done, 1)
            act.wait_ge(node_init, 1)
            half = E // 32 * 16
            act.dma_start(attr_rows[0:half, :].rearrange("(a b) f -> a (b f)", a=16), edge_attr[0:half, :].rearrange("(a b) f -> a (b f)", a=16)).then_inc(attr_copied, 16)
            act.dma_start(attr_rows[half:E, :].rearrange("(a b) f -> a (b f)", a=16), edge_attr[half:E, :].rearrange("(a b) f -> a (b f)", a=16)).then_inc(attr_copied, 16)
            for r0 in range(E, EP, 64):
                act.dma_start(attr_rows[r0:r0 + 64, :], zeros[0:64, 0:D]).then_inc(attr_copied, 16)


            def copy_out(S, q, b, g):
                G = (q * 2 + b) * CG + g
                act.wait_ge(S.back_done, G + 1 + FREE_G)
                nc.scalar.activation(rows_out[:, b, g * GT:(g + 1) * GT, :], back[:, g % 2, 0:GT * D].rearrange("p (t f) -> p t f", f=D), ACT.Copy).then_inc(S.out_copied, 1)

            def scale_steps(S, F, parts, dense_way):
                n_pairs = PAIRS - F
                act.sem_inc(S.scaled_done, FREE_G)
                act.sem_inc(S.out_copied, FREE_B)
                if dense_way:
                    act.sem_inc(S.out_turned, 1)
                for part, (k0, n_steps) in enumerate(parts):
                    with act.Fori(0, n_steps) as kk:
                        k = kk + k0

                        def pair(i, with_dense):
                            q = k * n_pairs + i
                            if with_dense:
                                act.wait_ge(S.dense_done, (k * D_ITERS + i) * (2 * UNIT_J) + FREE_R)
                                nc.scalar.activation(u_st[:, :], u_sb[:, bass.ds(i * (UNIT_J * D), UNIT_J * D)], ACT.Copy).then_inc(S.u_staged, 1)
                            for b in range(2):
                                act.wait_ge(S.gathered[part][b], (kk * n_pairs + i + 1) * (16 * CT))
                                act.wait_ge(S.fwd_done, (q * 2 + b) * CG + CG)
                                for g in range(CG):
                                    for t in range(g * GT, (g + 1) * GT):
                                        last = nc.scalar.activation(scaled[:, b, t, :], rows_in[:, b, t, :], ACT.Copy, scale=w_st[:, b, t:t + 1])
                                    last.then_inc(S.scaled_done, 1)
                                act.wait_ge(S.rows_stored[b], q * 16 + 16)
                                for g in range(CG):
                                    copy_out(S, q, b, g)

                        if dense_way:
                            wait_count(act, S.node_done, k * NODE_BLOCKS + 2)
                            with act.Fori(0, D_ITERS) as i:
                                pair(i, True)
                            act.wait_ge(S.acc_done, k + 1)
                            nc.scalar.activation(dense_sum.rearrange("p (b c) -> p b c", b=4), fwd[:, :, 0:DC], ACT.Copy).then_inc(S.sum_copied, 1)
                            for r in range(5):
                                act.wait_ge(S.turned, k * 5 + r + 1)
                                nc.scalar.activation(dense_out[0:NJ, r * 4:(r + 1) * 4, :, :].rearrange("p a t f -> p (a t f)"), fwd[0:NJ, r % 4, :], ACT.Copy).then_inc(S.out_turned, 1)
                            with act.Fori(D_ITERS, n_pairs) as i:
                                pair(i, False)
                        else:
                            with act.Fori(0, n_pairs) as i:
                                pair(i, False)

            way = choose(act)
            with act.If_eq(way, 0):
                scale_steps(S_DENSE, F_PAIR, FAST_PARTS, True)
            with act.Else():
                scale_steps(S_ALL, 0, ALL_PARTS, False)
            act.wait_ge(root_in, 2)
            nc.scalar.activation(stat[:, 0, :], stat[:, 1, :], ACT.Sqrt).then_inc(root_done, 1)
            with act.Fori(0, NODE_PAIRS) as j:
                for b in range(2):
                    n = j * 2 + b
                    act.wait_ge(x1T_done, n + 1)
                    act.wait_ge(kvq_done, n + 1)
                    nc.scalar.activation(xT[0:D, b, :, :].rearrange("p j n -> p (j n)"), x1T_ps[0:D, 0:NB * P], ACT.Copy).then_inc(x1T_copied, 1)

            def attr_copy(G, g):
                act.wait_ge(attrT_done, G + 1 + 2)
                act.wait_ge(eproj_done, G + 1)
                nc.scalar.activation(attrT[0:D, g % 2, :], fwd[0:D, g % 2, :], ACT.Copy).then_inc(attrT_copied, 1)

            act.sem_inc(S_ATT.out_copied, FREE_B)
            with act.Fori(0, PAIRS) as i:
                q = i
                attr_copy(i * (2 * CG), 0)
                for g in range(2 * CG):
                    G = i * (2 * CG) + g
                    if g + 1 < 2 * CG:
                        attr_copy(G + 1, g + 1)
                    act.wait_ge(clipped, G + 1)
                    nc.scalar.activation(score[:, g % 2, :, :], score[:, g % 2, :, :], ACT.Exp).then_inc(exp_done, 1)
                    if g % CG == 0:
                        act.wait_ge(S_ATT.rows_stored[g // CG], i * 16 + 16)
                    copy_out(S_ATT, q, g // CG, g % CG)
            act.wait_ge(root_in, 3)
            nc.scalar.activation(stat[:, 0, :], stat[:, 1, :], ACT.Sqrt).then_inc(root_done, 1)

        @block.vector
        def _(dve):
            v = nc.vector
            link = Chain(dve, vec_pre)
            dve.sem_inc(row_used, 2)
            v.memset(blank, 0.0).then_inc(blank_ready, 1)
            v.memset(dst_nat[:, QB - 1, :], NT)
            v.memset(src_nat[:, QB - 1, :], 0)
            v.memset(w_nat[:, QB - 1, :], 0.0)
            v.memset(prev_nat[:, QB - 1, :], 0)
            v.memset(h_sb[:, :], 0.0)
            link(v.memset(prev_nat[0:1, 0, 0:1], -1))
            v.memset(sums[:, 1, :], 0.0).then_inc(cleared, 1)
            dve.wait_ge(loaded_e, 16 * 14)
            v.tensor_copy(dst_f, dst_nat)
            v.tensor_copy(prev_f, prev_nat)
            link(v.tensor_copy(src_f, src_nat))
            dve.sem_inc(nat_ready, 1)
            v.tensor_tensor(same_nat, dst_f, prev_f, ALU.is_equal).then_inc(same_nat_ready, 1)
            DR = DQ - P
            v.memset(bad[:, :], 0.0)
            link(v.tensor_scalar(src_nf, dst_f, float(DN), None, ALU.is_ge))
            link(v.tensor_reduce(bad[:, 0:1], src_nf[:, 0, :], AX, ALU.add))
            link(v.tensor_reduce(bad[0:DR, 1:2], src_nf[0:DR, 1, :], AX, ALU.add))
            link(v.tensor_tensor(bad[:, 0:1], bad[:, 0:1], bad[:, 1:2], ALU.add))
            dve.sem_inc(bad_ready, 1)
            dve.wait_ge(bad_summed, 1)
            v.tensor_scalar(flag[:, :], back[0:1, 0, 0:1], 0.0, None, ALU.is_gt).then_inc(flag_ready, 1)
            n = 0
            for a, to in ((0, src_pf), (1, dst_pf), (2, w_p[:, 0:NT_TILES])):
                to_v = to.rearrange("p (q u) -> p u q", u=GT)
                for r in range(QB):
                    rows = min(P, NQ - r * P)
                    dve.wait_ge(nat_T, n + 1)
                    link(v.tensor_copy(to_v[:, :, r * P:r * P + rows], fwd[:, n % 4, :].rearrange("p (u q) -> p u q", u=GT)[:, :, 0:rows]))
                    dve.sem_inc(nat_T_used, 1)
                    n += 1
            v.tensor_copy(src_idx[:, 0:NT_TILES], src_pf)
            link(v.tensor_scalar(dst_idx[:, 0:NT_TILES], dst_pf, float(NT - 1), None, ALU.min))
            dve.sem_inc(nat_T_all, 1)
            link(v.tensor_scalar(dense_idx[:, :], src_idx[:, 0:DT], DENSE_PITCH.bit_length() - 1, None, ALU.logical_shift_left))
            link(v.tensor_tensor(dense_idx[:, :], dense_idx[:, :], dst_idx[:, 0:DT], ALU.bitwise_or))
            dve.sem_inc(add_used, 2)
            for f, hi, lo in ((src_pf, src_hi, src_lo), (dst_pf, dst_hi, dst_lo)):
                link(v.tensor_scalar(hi, f, 1.0 / NJ, 0.5 / NJ - 0.5, ALU.mult, ALU.add))
                link(v.tensor_scalar(hi, hi, ROUND, None, ALU.add))
                link(v.tensor_scalar(hi, hi, ROUND, None, ALU.subtract))
                link(v.scalar_tensor_tensor(lo, hi, -float(NJ), f, ALU.mult, ALU.add))
            dve.wait_ge(same_stored, 32)
            link(v.memset(x_sb[96:P, :], 0.0))
            dve.sem_inc(cleared, 1)
            def add_half(i, b):
                h = i * 2 + b
                chain = Chain(dve, vec_add, h * 6)
                dve.wait_ge(row_loaded[b], i * 48 + 48)
                tiles = bass.ds(i * 16 + b * 8, 8)

                def row(a, t):
                    z = row_in[:, b, a, :].rearrange("p (g e u) -> p g u e", g=2, u=GT)[:, t // GT, t % GT, :]
                    return z if a == 2 else z.bitcast(I32)

                def col(of, t):
                    return of[:, bass.ds(i * 16 + (b * 8 + t), 1)]

                for t in range(8):
                    last = v.tensor_scalar(eq_src[:, t, :], row(0, t), col(src_pf, t), None, ALU.is_equal)
                chain(last)
                for t in range(8):
                    last = v.scalar_tensor_tensor(eq_both[:, t, :], row(1, t), col(dst_pf, t), eq_src[:, t, :], ALU.is_equal, ALU.mult)
                chain(last)
                dve.wait_ge(add_used, h + 1)
                for t in range(8):
                    v.tensor_tensor_reduce(out=eq_junk[:, t, :], in0=eq_both[:, t, :], in1=row(2, t), scale=1.0, scalar=0.0,
                                           op0=ALU.mult, op1=ALU.add, accum_out=add_w[:, b, t:t + 1])
                    last = v.tensor_tensor_reduce(out=eq_src[:, t, :], in0=eq_both[:, t, :], in1=earlier[:, :], scale=1.0, scalar=0.0,
                                                  op0=ALU.mult, op1=ALU.add, accum_out=repeats[:, t:t + 1])
                chain(last)
                dve.sem_inc(row_used, 1)
                chain(v.tensor_scalar(add_idx[:, b, :], repeats[:, :], 0.0, float(DENSE_PITCH - 1), ALU.is_gt, ALU.mult))
                chain(v.tensor_tensor(add_idx[:, b, :], add_idx[:, b, :], dense_idx[:, tiles], ALU.bitwise_or))
                chain(v.tensor_copy(repeats[:, 0:1], repeats[:, 0:1]))
                dve.sem_inc(add_ready, 1)

            def one_hots(i, n):
                dve.wait_ge(hots_used, i * 8 + n + 1)
                for t in range(HB):
                    at = bass.ds(i * (8 * HB) + (n * HB + t), 1)
                    o = hots[:, n % 2, t, :]
                    v.tensor_scalar(o[:, 0:P], iota_p[:, :], dst_hi[:, at], None, ALU.is_equal)
                    v.tensor_scalar(o[:, P:P + NJ], iota_j[:, :], dst_lo[:, at], w_p[:, at], ALU.is_equal, ALU.mult)
                    v.tensor_scalar(o[:, P + NJ:P + 2 * NJ], iota_j[:, :], dst_lo[:, at], None, ALU.is_equal)
                    v.tensor_scalar(o[:, P + 2 * NJ:2 * P + 2 * NJ], iota_p[:, :], src_hi[:, at], None, ALU.is_equal)
                    last = v.tensor_scalar(o[:, 2 * P + 2 * NJ:HOT], iota_j[:, :], src_lo[:, at], w_p[:, at], ALU.is_equal, ALU.mult)
                last.then_inc(hots_ready, 1)

            HOT_ITERS = NT_TILES // (8 * HB)
            assert HOT_ITERS * 8 * HB == NT_TILES and HOT_ITERS < DH8 // 2
            with dve.Fori(0, HOT_ITERS) as i:
                for b in range(2):
                    add_half(i, b)
                    for n in range(4):
                        one_hots(i, 4 * b + n)
            with dve.Fori(HOT_ITERS, DH8 // 2) as i:
                for b in range(2):
                    add_half(i, b)
            dve.wait_ge(counted, 1)
            v.tensor_scalar(deg[:, 1, :], back[:, 0, 0:NJ], 1.0, None, ALU.add)
            v.tensor_copy(count[:, :], back[:, 0, NJ:2 * NJ])
            link(v.tensor_scalar(deg[:, 0, :], back[:, 1, 0:NJ], 1.0, None, ALU.add))
            v.tensor_scalar(inv_out[:, :], deg[:, 0, :], 0.0, None, ALU.is_gt)
            link(v.tensor_scalar(inv_in9[:, :], deg[:, 1, :], 0.0, 1.0 - ALPHA, ALU.is_gt, ALU.mult))
            link(v.tensor_scalar(deg[:, 0:2, :], deg[:, 0:2, :], 1e-30, None, ALU.max))
            dve.sem_inc(root_in, 1)
            dve.wait_ge(root_done, 1)
            r2, t2, d2 = deg_t[:, 0:2, :], stat[:, :, :], deg[:, 0:2, :]
            link(v.reciprocal(r2, r2))
            link(v.tensor_tensor(t2, r2, r2, ALU.mult))
            link(v.tensor_tensor(t2, t2, d2, ALU.mult))
            link(v.tensor_scalar(t2, t2, -0.5, 1.5, ALU.mult, ALU.add))
            link(v.tensor_tensor(r2, r2, t2, ALU.mult))
            v.tensor_tensor(inv_out[:, :], inv_out[:, :], deg_t[:, 0, :], ALU.mult)
            v.tensor_tensor(inv_in9[:, :], inv_in9[:, :], deg_t[:, 1, :], ALU.mult)
            link(v.tensor_tensor_scan(deg[:, 2, :], ones[:, :], count[:, :], 0.0, ALU.mult, ALU.add))
            link(v.tensor_copy(first[:, :], deg[:, 2, NJ - 1:NJ]))
            dve.sem_inc(totals_ready, 1)
            dve.wait_ge(offsets_ready, 1)
            link(v.tensor_copy(first[:, :], proj[:, 0, 0:1]))
            link(v.tensor_scalar(deg[:, 2, :], deg[:, 2, :], first[:, 0:1], float(-1 - ZERO_ROW), ALU.add, ALU.add))
            link(v.tensor_scalar(deg_t[:, 2, :], count[:, :], 0.0, None, ALU.is_gt))
            link(v.tensor_tensor(deg[:, 2, :], deg[:, 2, :], deg_t[:, 2, :], ALU.mult))
            link(v.tensor_scalar(end_idx[:, 0:NJ], deg[:, 2, :], float(ZERO_ROW), None, ALU.add))
            v.tensor_copy(all_ends[:, :], end_idx[:, 0:NJ])
            link(v.tensor_copy(end_idx[:, NJ:NJ + 2 * NB], end_idx[:, 0:2 * NB]))
            dve.wait_ge(loaded_x, 32)
            link(v.tensor_tensor(u_sb[:, :].rearrange("p (j f) -> p j f", f=D), x_sb[:, :].rearrange("p (j f) -> p j f", f=D),
                                 inv_out[:, :].unsqueeze(2).broadcast_to([P, NJ, D]), ALU.mult))
            dve.sem_inc(node_init, 1)

            def stage(S, b, at):
                v.tensor_copy(src_st[:, b, :], src_idx[:, at])
                v.tensor_copy(dst_st[:, b, :], dst_idx[:, at])
                v.tensor_copy(w_st[:, b, :], w_p[:, at]).then_inc(S.staged, 1)

            def stage_first(S, F):
                start = Chain(dve, S.vec_first, 6 if F else 0)
                W, f = WRAP * GT, F * 2 * CT
                for a in (src_idx, dst_idx, w_p):
                    last = v.tensor_copy(a[:, NT_TILES:NT_TILES + W], a[:, f:f + W])
                start(last)
                for b in range(2):
                    stage(S, b, slice(f + b * CT, f + (b + 1) * CT))
                    v.tensor_copy(end_st[:, b, :], end_idx[:, b * NB:(b + 1) * NB]).then_inc(S.end_staged, 1)
                dve.sem_inc(S.scan_done, FREE_F)
                dve.sem_inc(S.node_done, 2)

            def scan(S, q, b, g, bank):
                G = (q * 2 + b) * CG + g
                dve.wait_ge(S.fwd_done, G + 1 + FREE_G)
                dve.wait_ge(S.back_done, G + 1)
                if g == 0:
                    dve.wait_ge(S.same_ready[b], (q + 1) * 16)
                    before = sums[0:D, 1 - b, CE - 1:CE]
                else:
                    before = sums[0:D, b, g * GE - 1:g * GE]
                dve.wait_ge(S.scan_done, G + FREE_F)
                v.tensor_tensor_scan(sums[0:D, b, g * GE:(g + 1) * GE], same[:, b, g * GE:(g + 1) * GE],
                                     bank, before, ALU.mult, ALU.add).then_inc(S.scan_done, 1)

            def sum_steps(S, F, parts, dense_way):
                n_pairs = PAIRS - F
                per_block = 5 if dense_way else 4
                if dense_way:
                    link = Chain(dve, S.vec_first)
                    end_f, late = deg[:, 2, :], deg_t[:, 2, :]
                    link(v.tensor_copy(end_f, end_idx[:, 0:NJ]))
                    link(v.tensor_scalar(late, end_f, float(DE), None, ALU.is_ge))
                    link(v.tensor_scalar(end_f, end_f, float(-ZERO_ROW), None, ALU.add))
                    link(v.tensor_tensor(end_f, end_f, late, ALU.mult))
                    link(v.tensor_scalar(end_idx[:, 0:NJ], end_f, float(ZERO_ROW - DE), None, ALU.add))
                    link(v.tensor_copy(end_idx[:, NJ:NJ + 2 * NB], end_idx[:, 0:2 * NB]))
                stage_first(S, F)
                for k0, n_steps in parts:
                    final = k0 == STEPS - 1
                    with dve.Fori(0, n_steps) as kk:
                        k = kk + k0
                        with dve.Fori(0, n_pairs) as i:
                            for b in range(2):
                                for g in range(CG):
                                    scan(S, k * n_pairs + i, b, g, proj[0:D, g % 2, :])
                                stage(S, b, bass.ds(i * (2 * CT) + (2 * F + b + 2) * CT, CT))
                        if dense_way:
                            wait_count(dve, S.dense_loaded, k * 16 + 16)
                        with dve.Fori(0, NODE_PAIRS) as j:
                            for b in range(2):
                                blk = k * NODE_PAIRS + j
                                step = Chain(dve, S.vec_node, (blk * 2 + b) * per_block)
                                dve.wait_ge(S.ends_gathered[b], (blk + 1) * (16 * NB))
                                cols = bass.ds((j * 2 + b) * (NB * D), NB * D)
                                nodes = bass.ds((j * 2 + b) * NB, NB)
                                e3 = ends_in[:, b, :, :]
                                e2 = e3.rearrange("p j f -> p (j f)")
                                step(v.tensor_tensor(e2, e2, u_sb[:, cols], ALU.add))
                                if dense_way:
                                    ed = e2[0:NODE_DENSE]
                                    step(v.tensor_tensor(ed, ed, dense_n[0:NODE_DENSE, cols], ALU.add))
                                step(v.tensor_tensor(e3, e3, inv_in9[:, nodes].unsqueeze(2).broadcast_to([P, NB, D]), ALU.mult))
                                if final:
                                    step(v.scalar_tensor_tensor(u_sb[:, cols], x_sb[:, cols], ALPHA, e2, ALU.mult, ALU.add))
                                    step(v.tensor_copy(e2[:, 0:1], e2[:, 0:1]))
                                else:
                                    step(v.scalar_tensor_tensor(e2, x_sb[:, cols], ALPHA, e2, ALU.mult, ALU.add))
                                    step(v.tensor_tensor(u_sb[:, cols].rearrange("p (j f) -> p j f", f=D), e3, inv_out[:, nodes].unsqueeze(2).broadcast_to([P, NB, D]), ALU.mult))
                                dve.sem_inc(S.node_done, 1)
                                v.tensor_copy(end_st[:, b, :], end_idx[:, bass.ds((j * 2 + b + 2) * NB, NB)]).then_inc(S.end_staged, 1)
                dve.wait_ge(S.node_stored, STEPS * (16 * NODE_BLOCKS) + 16)

            way = choose(dve)
            with dve.If_eq(way, 0):
                sum_steps(S_DENSE, F_PAIR, FAST_PARTS, True)
            with dve.Else():
                sum_steps(S_ALL, 0, ALL_PARTS, False)

            norm = Chain(dve, vec_ln)

            def layernorm(o, s, t, nth):
                s3, t3, o3 = (z[:, :].rearrange("p (j f) -> p j f", f=D) for z in (s, t, o))
                norm(v.tensor_reduce(stat[:, 0, :], s3, AX, ALU.add))
                norm(v.tensor_scalar(stat[:, 0, :], stat[:, 0, :], 1.0 / D, None, ALU.mult))
                norm(v.tensor_tensor(s3, s3, stat[:, 0, :].unsqueeze(2).broadcast_to([P, NJ, D]), ALU.subtract))
                norm(v.tensor_tensor(t3, s3, s3, ALU.mult))
                norm(v.tensor_reduce(stat[:, 1, :], t3, AX, ALU.add))
                norm(v.tensor_scalar(stat[:, 1, :], stat[:, 1, :], 1.0 / D, EPS, ALU.mult, ALU.add))
                dve.sem_inc(root_in, 1)
                dve.wait_ge(root_done, nth)
                norm(v.reciprocal(stat[:, 1, :], stat[:, 0, :]))
                norm(v.tensor_tensor(o3, s3, stat[:, 1, :].unsqueeze(2).broadcast_to([P, NJ, D]), ALU.mult))

            norm(v.tensor_copy(end_idx[:, 0:NJ], all_ends[:, :]))
            norm(v.tensor_copy(end_idx[:, NJ:NJ + 2 * NB], end_idx[:, 0:2 * NB]))
            norm(v.tensor_tensor(h_sb[:, :], u_sb[:, :], x_sb[:, :], ALU.add))
            layernorm(x_sb, h_sb, tmp, 2)
            v.memset(u_sb[D:D + 1, :], 1.0).then_inc(ones_row, 1)

            with dve.Fori(0, NODE_PAIRS) as j:
                for b in range(2):
                    n = j * 2 + b
                    v.tensor_copy(x_st[:, b, :, :].rearrange("p j f -> p (j f)"), x_sb[:, bass.ds(n * (NB * D), NB * D)]).then_inc(x1_staged, 1)
                    dve.wait_ge(kvq_done, n + 1 + 2)
                    for r in range(NB // 2):
                        last = v.tensor_copy(kvq_out[:, b, 2 * r:2 * r + 2, :].rearrange("p j f -> p (j f)"), kvq_ps(r)[:, 0:2 * 3 * D])
                    last.then_inc(kvq_copied, 1)
                for b in range(2):
                    dve.wait_ge(kvq_stored[b], (j + 1) * 32)

            for b in range(2):
                dve.wait_ge(kvq_stored[b], 32 * NODE_PAIRS)
            isd = float(1.0 / float(DH) ** 0.5)
            stage_first(S_ATT, 0)
            EC = 6
            with dve.Fori(0, PAIRS) as i:
                q = i
                for b in range(2):
                    dve.wait_ge(S_ATT.gathered[0][b], (i + 1) * (32 * CT))
                    for g in range(CG):
                        Gl = (i * 2 + b) * CG + g
                        edge = Chain(dve, vec_edge, Gl * EC)
                        t0, t1 = g * GT, (g + 1) * GT
                        k4, v4, q4 = kv_in[:, b, t0:t1, 0:D], kv_in[:, b, t0:t1, D:2 * D], rows_in[:, b, t0:t1, :]
                        s4 = score[:, g % 2, :, :]
                        p4 = prod[:, g % 2, :, :]
                        edge(v.tensor_tensor(p4, k4, q4, ALU.mult))
                        dve.wait_ge(eproj_done, Gl + 1 + 2)
                        edge(v.tensor_tensor(p4, p4, proj[:, g % 2, 0:GT * D].rearrange("p (t f) -> p t f", f=D), ALU.mult))
                        edge(v.tensor_reduce(s4, p4.rearrange("p t (h d) -> p t h d", d=DH), AX, ALU.add))
                        edge(v.tensor_scalar(s4, s4, isd, 5.0, ALU.mult, ALU.min))
                        edge(v.tensor_scalar(s4, s4, -5.0, None, ALU.max))
                        dve.sem_inc(clipped, 1)
                        dve.wait_ge(exp_done, Gl + 1)
                        dve.wait_ge(S_ATT.fwd_done, Gl + FREE_G - 3)
                        edge(v.tensor_tensor(msg[:, g, :, :].rearrange("p t (h d) -> p t h d", d=DH), v4.rearrange("p t (h d) -> p t h d", d=DH),
                                             s4.unsqueeze(3).broadcast_to([P, GT, HEADS, DH]), ALU.mult))
                        dve.sem_inc(kv_used, 1)
                        scan(S_ATT, q, b, g, fwd[0:D, 2 + g % 2, :])
                    stage(S_ATT, b, bass.ds(i * (2 * CT) + (b + 2) * CT, CT))
            with dve.Fori(0, NODE_PAIRS) as j:
                for b in range(2):
                    dve.wait_ge(S_ATT.ends_gathered[b], (j + 1) * (16 * NB))
                    cols = bass.ds((j * 2 + b) * (NB * D), NB * D)
                    v.tensor_tensor(h_sb[:, cols], ends_in[:, b, :, :].rearrange("p j f -> p (j f)"), x_sb[:, cols], ALU.add).then_inc(S_ATT.node_done, 1)
                    v.tensor_copy(end_st[:, b, :], end_idx[:, bass.ds((j * 2 + b + 2) * NB, NB)]).then_inc(S_ATT.end_staged, 1)
            dve.wait_ge(S_ATT.node_done, 2 + NODE_BLOCKS)
            layernorm(h_sb, h_sb, tmp, 3)
            dve.sem_inc(y_done, 1)

        @block.tensor
        def _(pe):
            for S in (S_DENSE, S_ALL, S_ATT):
                pe.sem_inc(S.fwd_done, FREE_G)
                pe.sem_inc(S.back_done, FREE_G)
            pe.sem_inc(S_DENSE.dense_done, FREE_R)
            pe.sem_inc(hots_used, 2)
            pe.sem_inc(attrT_done, 2)
            pe.sem_inc(eproj_done, 2)
            pe.sem_inc(kvq_done, 2)
            pe.sem_inc(kv_used, FREE_G)
            pe.wait_ge(consts, 3)
            pe.wait_ge(bad_ready, 1)
            nc.tensor.matmul(back[0:1, 0, 0:1], bad[:, 0:1], ones[:, 0:1], start=True, stop=True).then_inc(bad_summed, 1)
            pe.wait_ge(nat_ready, 1)
            n = 0
            for nat in (src_f, dst_f, w_nat):
                for r in range(QB):
                    rows = min(P, NQ - r * P)
                    if n >= 4:
                        pe.wait_ge(nat_T_used, n - 3)
                    for u in range(GT):
                        last = nc.tensor.transpose(fwd[:, n % 4, u * P:u * P + rows], nat[0:rows, r, u::GT], ident[0:rows, 0:rows])
                    last.then_inc(nat_T, 1)
                    n += 1
            pe.wait_ge(flag_ready, 1)
            nc.tensor.matmul(back[:, 0, 0:2 * NJ], zeros[:, 0:P], zeros[:, 0:2 * NJ], start=True, stop=False)
            nc.tensor.matmul(back[:, 1, 0:NJ], zeros[:, 0:P], zeros[:, 0:NJ], start=True, stop=False)
            with pe.Fori(0, NT_TILES // (2 * HB)) as i:
                for b in range(2):
                    wait_count(pe, hots_ready, i * 2 + b + 1)
                    for t in range(HB):
                        o = hots[:, b, t, :]
                        nc.tensor.matmul(back[:, 0, 0:2 * NJ], o[:, 0:P], o[:, P:P + 2 * NJ], start=False, stop=False)
                        last = nc.tensor.matmul(back[:, 1, 0:NJ], o[:, P + 2 * NJ:2 * P + 2 * NJ], o[:, 2 * P + 2 * NJ:HOT], start=False, stop=False)
                    last.then_inc(hots_used, 1)
            nc.tensor.matmul(back[:, 0, 0:2 * NJ], zeros[:, 0:P], zeros[:, 0:2 * NJ], start=False, stop=True)
            nc.tensor.matmul(back[:, 1, 0:NJ], zeros[:, 0:P], zeros[:, 0:NJ], start=False, stop=True).then_inc(counted, 1)
            pe.wait_ge(totals_ready, 1)
            nc.tensor.matmul(proj[:, 0, 0:1], lower[:, :], first[:, 0:1], start=True, stop=True).then_inc(offsets_ready, 1)

            def turn_back(S, q, b, g):
                G = (q * 2 + b) * CG + g
                wait_count(pe, S.scan_done, G + 1 + FREE_F)
                wait_count(pe, S.out_copied, G + 1)
                for u in range(GT):
                    last = nc.tensor.transpose(back[:, g % 2, u * D:(u + 1) * D], sums[0:D, b, g * GE + u:(g + 1) * GE:GT], ident[0:D, 0:D])
                last.then_inc(S.back_done, 1)

            def clear_sums(first_of, last_of):
                for bank in range(4):
                    for t in range(2):
                        last = nc.tensor.matmul(fwd[t * D:(t + 1) * D, bank, 0:DC], zeros[:, 0:D], zeros[:, 0:DC], start=first_of, stop=last_of, tile_position=(0, t * D))
                return last

            def multiply_unit(S, k, i, n):
                half, jj = n // UNIT_J, n % UNIT_J
                wait_count(pe, S.ring_ready[jj], (k * D_ITERS + i) * 32 + (half + 1) * 16)
                for gg in range(2):
                    for t in range(2):
                        last = nc.tensor.matmul(fwd[t * D:(t + 1) * D, half * 2 + gg, 0:DC], u_st[:, jj * D:(jj + 1) * D],
                                                ring[:, jj, t, gg * DC:(gg + 1) * DC], start=False, stop=False, tile_position=(0, t * D))
                last.then_inc(S.dense_done, 1)

            def turn_steps(S, F, parts, dense_way):
                n_pairs = PAIRS - F
                for k0, n_steps in parts:
                    with pe.Fori(0, n_steps) as kk:
                        k = kk + k0

                        def pair(i, with_dense):
                            q = k * n_pairs + i
                            n = 0
                            if with_dense:
                                wait_count(pe, S.u_staged, k * D_ITERS + i + 1)
                            for b in range(2):
                                for g in range(CG):
                                    G = (q * 2 + b) * CG + g
                                    wait_count(pe, S.scaled_done, G + 1 + FREE_G)
                                    wait_count(pe, S.scan_done, G + 1)
                                    for u in range(GT):
                                        last = nc.tensor.transpose(proj[0:D, g % 2, u::GT], scaled[:, b, g * GT + u, :], ident[:, :])
                                    last.then_inc(S.fwd_done, 1)
                                    if with_dense:
                                        for _ in range(1 + (g == CG - 1)):
                                            multiply_unit(S, k, i, n)
                                            n += 1
                                    if g > 0:
                                        turn_back(S, q, b, g - 1)
                                turn_back(S, q, b, CG - 1)

                        if dense_way:
                            wait_count(pe, S.out_turned, k * 5 + 1)
                            clear_sums(True, False)
                            with pe.Fori(0, D_ITERS) as i:
                                pair(i, True)
                            clear_sums(False, True).then_inc(S.acc_done, 1)
                            wait_count(pe, S.sum_copied, k + 1)
                            for r in range(5):
                                if r >= 4:
                                    wait_count(pe, S.out_turned, k * 5 + r - 2)
                                for a in range(4):
                                    at = (r * 4 + a) * NJ
                                    last = nc.tensor.transpose(fwd[0:NJ, r % 4, a * P:(a + 1) * P], dense_sum[:, at:at + NJ], ident[:, :])
                                last.then_inc(S.turned, 1)
                            with pe.Fori(D_ITERS, n_pairs) as i:
                                pair(i, False)
                        else:
                            with pe.Fori(0, n_pairs) as i:
                                pair(i, False)

            way = choose(pe)
            with pe.If_eq(way, 0):
                turn_steps(S_DENSE, F_PAIR, FAST_PARTS, True)
            with pe.Else():
                turn_steps(S_ALL, 0, ALL_PARTS, False)

            pe.wait_ge(loaded_w, 16 * 8)
            pe.wait_ge(ones_row, 1)
            with pe.Fori(0, NODE_PAIRS) as j:
                for b in range(2):
                    n = j * 2 + b
                    wait_count(pe, x1_staged, n + 1)
                    for t in range(NB):
                        last = nc.tensor.transpose(x1T_ps[0:D, t * P:(t + 1) * P], x_st[:, b, t, :], ident[:, :])
                    last.then_inc(x1T_done, 1)
                    wait_count(pe, x1T_copied, n + 1)
                    for t in range(NB):
                        last = nc.tensor.matmul(kvq_ps(t // 2)[:, (t % 2) * 3 * D:(t % 2 + 1) * 3 * D], xT[:, b, t, :], w_kvq[:, :], start=True, stop=True)
                    last.then_inc(kvq_done, 1)
                    wait_count(pe, kvq_copied, n + 1)

            def attr(G, g):
                b = g // CG
                if g % CG == 0:
                    wait_count(pe, attr_loaded[b], (i + 1) * 16)
                for u in range(GT):
                    last = nc.tensor.transpose(fwd[0:D, g % 2, u * P:(u + 1) * P], attr_in[:, b, (g % CG) * GT + u, :], ident[:, :])
                last.then_inc(attrT_done, 1)
                wait_count(pe, attrT_copied, G + 1)
                for u in range(GT):
                    last = nc.tensor.matmul(proj[:, g % 2, u * D:(u + 1) * D], attrT[:, g % 2, u * P:(u + 1) * P], w_e[:, :], start=True, stop=True)
                last.then_inc(eproj_done, 1)

            with pe.Fori(0, PAIRS) as i:
                q = i
                attr(i * (2 * CG), 0)
                for g in range(2 * CG):
                    Gl = i * (2 * CG) + g
                    if g + 1 < 2 * CG:
                        attr(Gl + 1, g + 1)
                    wait_count(pe, kv_used, Gl + 1 + FREE_G)
                    for u in range(GT):
                        last = nc.tensor.transpose(fwd[0:D, 2 + g % 2, u::GT], msg[:, g % CG, u, :], ident[:, :])
                    last.then_inc(S_ATT.fwd_done, 1)
                    turn_back(S_ATT, q, g // CG, g % CG)


_INS = ['x', 'src', 'dst', 'edge_attr_64', 'edge_weight', 'L1_gnn_WQ', 'L1_gnn_bQ', 'L1_gnn_WK', 'L1_gnn_bK',
        'L1_gnn_WE', 'L1_gnn_bE', 'L1_gnn_WV', 'L1_gnn_bV']
_OUTS = [((12500, 64), 'float32')]


def kernel(**inputs):
    import numpy as _np
    import concourse.bacc as _bacc
    from concourse import mybir as _mybir
    from concourse.bass_utils import run_bass_kernel_spmd as _run

    nc = _bacc.Bacc("TRN2", target_bir_lowering=False, num_devices=1)
    arrays, args = {}, []
    for name in _INS:
        a = _np.ascontiguousarray(inputs[name])
        arrays[f"in_{name}_dram"] = a
        args.append(nc.dram_tensor(f"in_{name}_dram", a.shape, _mybir.dt.from_np(a.dtype), kind="ExternalInput").ap())
    for i, (shape, dtype) in enumerate(_OUTS):
        dt = _mybir.dt.from_np(_np.dtype(dtype))
        args.append(nc.dram_tensor(f"out_{i}_dram", shape, dt, kind="ExternalOutput").ap())
    build(nc, *args)
    r = _run(nc, [arrays], core_ids=[0])
    got = tuple(r.results[0][f"out_{i}_dram"] for i in range(len(_OUTS)))
    return got[0]
```

```python
from contextlib import ExitStack

import concourse.bass as bass
from concourse import mybir

F32 = mybir.dt.float32
BF16 = mybir.dt.bfloat16
I32 = mybir.dt.int32
U32 = mybir.dt.uint32
ALU = mybir.AluOpType
ACT = mybir.ActivationFunctionType
AX = mybir.AxisListType.X

P = 128
STEPS = 10
ALPHA = 0.1
EPS = 1e-5
HEADS = 8
GT = 4
GE = GT * P
CG = 4
CT = CG * GT
CE = CG * GE
NB = 10
POS_DENSE = 25
NODE_DENSE = 34
DENSE_PITCH = 4096
ROUND = 12582912.0


class Chain:

    def __init__(self, eng, sem, base=0):
        self.eng, self.sem, self.base, self.n = eng, sem, base, 0

    def __call__(self, ins):
        self.n += 1
        ins.then_inc(self.sem, 1)
        self.eng.wait_ge(self.sem, self.base + self.n)


def build(nc, x, src, dst, edge_attr, edge_weight, WQ, bQ, WK, bK, WE, bE, WV, bV, out):
    N, D = x.shape
    E = src.shape[0]
    DH = D // HEADS
    NJ = -(-N // P // (2 * NB)) * 2 * NB
    NP = N // NJ
    assert NP * NJ == N and NP <= P
    assert NJ % (2 * NB) == 0 and D == 64 and DH * HEADS == D
    NT = P * NJ
    NCH = -(-E // CE)
    assert NCH % 2 == 0
    PAIRS = NCH // 2
    EP = NCH * CE
    NQ = EP // GE
    QB = -(-NQ // P)
    NT_TILES = NQ * GT
    WRAP = 2 * CG
    NODE_PAIRS = NJ // (2 * NB)
    NODE_BLOCKS = 2 * NODE_PAIRS
    F_PAIR = POS_DENSE
    DE = F_PAIR * 2 * CE
    DN = NODE_DENSE * NJ
    DQ = DE // GE
    DT = DE // P
    STREAMS = 4
    RG = DQ // STREAMS
    FAR = RG - 2
    UNIT_J = 5
    D_ITERS = NJ // UNIT_J
    DC = DN // 8
    SLOTS = UNIT_J
    HALF_P = NODE_DENSE // 2
    TURNS = -(-HALF_P // 4)
    assert DC <= 512 and DN % 8 == 0 and D_ITERS < PAIRS - F_PAIR and DQ == RG * STREAMS and RG % 2 == 0 and DE < E and DN < DENSE_PITCH - 1
    FAST_PARTS = [(0, STEPS - 1), (STEPS - 1, 1)]
    ALL_PARTS = [(0, 5), (5, STEPS - 6), (STEPS - 1, 1)]
    for first_pair, parts in ((F_PAIR, FAST_PARTS), (0, ALL_PARTS)):
        assert all(n * (PAIRS - first_pair) * 16 * CT < 65536 for _, n in parts)
    ZERO_ROW = EP
    QF = E // GE
    REST = E - QF * GE

    node_rows = nc.dram_tensor("node_rows", [NT, D], F32).ap()
    edge_rows = nc.dram_tensor("edge_rows", [EP + P, D], F32).ap()
    late_rows = nc.dram_tensor("late_rows", [EP - DE + P, D], F32).ap()
    same_rows = nc.dram_tensor("same_rows", [(NQ + WRAP) * GE], BF16).ap()
    dense = nc.dram_tensor("dense", [P * NJ * DENSE_PITCH, 1], F32).ap()
    dense_rows = nc.dram_tensor("dense_rows", [DN, D], F32).ap()
    attr_rows = nc.dram_tensor("attr_rows", [EP, D], F32).ap()
    kv_rows = nc.dram_tensor("kv_rows", [NT, 2 * D], F32).ap()
    q_starts = nc.dram_tensor("q_starts", [EP + NT, D], F32).ap()

    dense_v = dense.rearrange("(p j c) o -> p j (c o)", j=NJ, c=DENSE_PITCH)
    node_rows_v = node_rows.rearrange("(p j) f -> p (j f)", j=NJ)
    kv_rows_v = kv_rows.rearrange("(p j) f -> p j f", j=NJ)

    def sum_rows(F):
        return late_rows if F else edge_rows

    def by_group(rows):
        return rows[0:rows.shape[0] - P, :].rearrange("(g p u) f -> p g (u f)", p=P, u=GT)

    attr_rows_v = attr_rows.rearrange("(g p u) f -> p g u f", p=P, u=GT)
    q_starts_v = q_starts[0:EP, :].rearrange("(g p u) f -> p g u f", p=P, u=GT)

    with ExitStack() as ctx:
        def sb(name, shape, dt=F32):
            return ctx.enter_context(nc.sbuf_tensor(name, shape, dt))

        def sem(name):
            return ctx.enter_context(nc.semaphore(name))

        x_sb = sb("x_sb", [P, NJ * D])
        u_sb = sb("u_sb", [P, NJ * D])
        big = sb("big", [P, 2 * NJ * D])
        h_sb, tmp = big[:, 0:NJ * D], big[:, NJ * D:2 * NJ * D]
        ring = big[:, 0:SLOTS * 4 * DC].rearrange("p (s t c) -> p s t c", s=SLOTS, t=2)
        dense_sum = big[:, SLOTS * 4 * DC:SLOTS * 4 * DC + 4 * DC]
        dense_out = big[:, 0:NODE_DENSE * D].rearrange("p (a t f) -> p a t f", t=2, f=D)
        dense_n = big[:, NODE_DENSE * D:NODE_DENSE * D + NJ * D]
        src_idx = sb("src_idx", [P, (NQ + WRAP) * GT], I32)
        dst_idx = sb("dst_idx", [P, (NQ + WRAP) * GT], I32)
        w_p = sb("w_p", [P, (NQ + WRAP) * GT])
        end_idx = sb("end_idx", [P, NJ + 2 * NB], I32)
        rows_in = sb("rows_in", [P, 2, CT, D])
        scaled = sb("scaled", [P, 2, CT, D])
        sums = sb("sums", [P, 2, CE])
        same = sb("same", [P, 2, CE], BF16)
        rows_out = sb("rows_out", [P, 2, CT, D])
        u_st = sb("u_st", [P, UNIT_J * D])
        dense_idx = sb("dense_idx", [P, DT], I32)
        add_idx = sb("add_idx", [P, 2, STREAMS, GT], I32)
        add_w = sb("add_w", [P, 2, STREAMS, GT])
        repeats = sb("repeats", [P, 8])
        all_ends = sb("all_ends", [P, NJ], I32)
        flag = sb("flag", [1, 1], I32)
        bad = sb("bad", [P, 4])
        earlier = sb("earlier", [P, P])
        src_st = sb("src_st", [P, 2, CT], I32)
        w_st = sb("w_st", [P, 2, CT])
        end_st = sb("end_st", [P, 2, NB], I32)
        start_idx = sb("start_idx", [P, NJ], I32)
        start_st = sb("start_st", [P, 2, NB], I32)
        no_edges = sb("no_edges", [P, NJ])
        ends_in = sb("ends_in", [P, 2, NB, D])
        ident = sb("ident", [P, P])
        lower = sb("lower", [P, P])
        iota_p = sb("iota_p", [P, P])
        iota_j = sb("iota_j", [P, NJ])
        ones = sb("ones", [P, NJ])
        zeros = sb("zeros", [P, 512])
        inv_out = sb("inv_out", [P, NJ])
        inv_in9 = sb("inv_in9", [P, NJ])
        deg = sb("deg", [P, 3, NJ])
        deg_t = sb("deg_t", [P, 3, NJ])
        count = sb("count", [P, NJ])
        first = sb("first", [P, 1])
        w_kvq = sb("w_kvq", [D + 1, 3 * D])
        w_e = sb("w_e", [D + 1, D])
        stat = sb("stat", [P, 2, NJ])
        score = sb("score", [P, 2, GT, HEADS])

        nat_i = tmp[:, 0:3 * QB * GE].rearrange("p (a r i) -> p a r i", a=3, i=GE)
        src_nat, dst_nat = nat_i[:, 0].bitcast(I32), nat_i[:, 1].bitcast(I32)
        w_nat = nat_i[:, 2]
        nat_f = u_sb[:, 0:3 * QB * GE].rearrange("p (a r i) -> p a r i", a=3, i=GE)
        prev_nat, dst_f, prev_f = nat_f[:, 0].bitcast(I32), nat_f[:, 1], nat_f[:, 2]
        src_f = sums[:, :, :].rearrange("p a e -> p (a e)")[:, 0:QB * GE].rearrange("p (r i) -> p r i", i=GE)
        same_nat = x_sb[:, 0:QB * GE // 2].bitcast(BF16).rearrange("p (r i) -> p r i", i=GE)
        far_nat = rows_in[:, :, :, :].rearrange("p a t f -> p (a t f)")[:, 0:2 * GE].bitcast(I32).rearrange("p (r i) -> p r i", i=GE)
        far_eq = scaled[:, :, :, :].rearrange("p a t f -> p (a t f)")[:, 0:2 * GE].rearrange("p (r i) -> p r i", i=GE)
        src_nf = h_sb[:, 0:QB * GE].rearrange("p (r i) -> p r i", i=GE)
        src_pf = rows_in[:, :, :, :].rearrange("p a t f -> p (a t f)")[:, 0:NT_TILES]
        dst_pf = scaled[:, :, :, :].rearrange("p a t f -> p (a t f)")[:, 0:NT_TILES]
        digits = tmp[:, 0:4 * NT_TILES].rearrange("p (a t) -> p a t", a=4)
        src_hi, src_lo, dst_hi, dst_lo = (digits[:, a] for a in range(4))
        blank = rows_out[:, :, :, :].rearrange("p b t f -> p (b t f)")
        row_in = u_sb[:, 0:6 * 8 * P].rearrange("p (b a e) -> p b a e", b=2, a=3)
        eq_src = sums[:, 0, 0:8 * P].rearrange("p (t e) -> p t e", e=P)
        eq_both = sums[:, 0, 8 * P:16 * P].rearrange("p (t e) -> p t e", e=P)
        HOT = 2 * P + 3 * NJ
        HB = 4
        HOT_ITERS = NT_TILES // (8 * HB)
        hots = h_sb[:, 0:2 * HB * HOT].rearrange("p (b t c) -> p b t c", b=2, c=HOT)
        eq_junk = h_sb[:, 2 * HB * HOT:2 * HB * HOT + 8 * P].rearrange("p (t e) -> p t e", e=P)

        kvq_out = tmp[:, 0:2 * NB * 3 * D].rearrange("p (b j f) -> p b j f", b=2, f=3 * D)
        x_st = tmp[:, 2 * NB * 3 * D:2 * NB * 4 * D].rearrange("p (b j f) -> p b j f", b=2, f=D)
        xT = u_sb[0:D + 1, 0:2 * NB * P].rearrange("p (b j n) -> p b j n", b=2, n=P)
        kv_in = u_sb[:, 0:2 * CT * 2 * D].rearrange("p (b t f) -> p b t f", b=2, f=2 * D)
        attrT = u_sb[0:D + 1, 2 * CT * 2 * D:2 * CT * 2 * D + 2 * GE].rearrange("p (b e) -> p b e", b=2)
        attr_in = tmp[:, 0:4 * CT * D].rearrange("p (b t f) -> p b t f", b=2, f=2 * D)
        prod = tmp[:, 4 * CT * D:4 * CT * D + 2 * GT * D].rearrange("p (b t f) -> p b t f", b=2, f=D)
        msg = tmp[:, 4 * CT * D + 2 * GT * D:4 * CT * D + 6 * GT * D].rearrange("p (b t f) -> p b t f", b=4, f=D)

        x1_ps_all = ctx.enter_context(nc.psum_tensor("banks", [P, 8, GE], F32))
        fwd, back, proj = x1_ps_all[:, 0:4, :], x1_ps_all[:, 4:6, :], x1_ps_all[:, 6:8, :]

        x1T_ps = x1_ps_all[:, 5:8, :].rearrange("p b e -> p (b e)")

        def kvq_ps(r):
            return x1_ps_all[:, r, :]

        loaded_e = sem("loaded_e")
        loaded_x = sem("loaded_x")
        loaded_w = sem("loaded_w")
        attr_copied = sem("attr_copied")
        cleared = sem("cleared")
        consts = sem("consts")
        vec_pre = sem("vec_pre")
        vec_node = sem("vec_node")
        vec_ln = sem("vec_ln")
        vec_edge = sem("vec_edge")
        nat_ready = sem("nat_ready")
        same_nat_ready = sem("same_nat_ready")
        same_stored = sem("same_stored")
        nat_T = sem("nat_T")
        nat_T_used = sem("nat_T_used")
        hots_plain = sem("hots_plain")
        hots_ready = sem("hots_ready")
        hots_used = sem("hots_used")
        counted = sem("counted")
        root_in = sem("root_in")
        root_done = sem("root_done")
        totals_ready = sem("totals_ready")
        offsets_ready = sem("offsets_ready")
        node_init = sem("node_init")
        dense_cleared = sem("dense_cleared")
        nat_T_all = sem("nat_T_all")
        row_loaded = [sem("row_loaded0"), sem("row_loaded1")]
        row_used = sem("row_used")
        add_ready = sem("add_ready")
        add_used = sem("add_used")
        added = [sem(f"added{s}") for s in range(STREAMS)]
        vec_add = sem("vec_add")
        bad_ready = sem("bad_ready")
        bad_summed = sem("bad_summed")
        flag_ready = sem("flag_ready")

        class EdgeSems:

            def __init__(self, name, parts, slots=0):
                def one(what):
                    return sem(f"{what}_{name}")

                def pair(what):
                    return [sem(f"{what}_{name}{b}") for b in range(2)]

                self.staged = one("staged")
                self.gathered = [pair(f"gathered{part}") for part in range(parts)]
                self.scaled_done = one("scaled_done")
                self.fwd_done = one("fwd_done")
                self.same_ready = pair("same_ready")
                self.scan_done = one("scan_done")
                self.back_done = one("back_done")
                self.out_copied = one("out_copied")
                self.rows_stored = pair("rows_stored")
                self.end_staged = one("end_staged")
                self.ends_gathered = pair("ends_gathered")
                self.node_done = one("node_done")
                self.node_stored = one("node_stored")
                self.vec_first = one("vec_first")
                self.vec_node = one("vec_node")
                self.restarted = one("restarted")
                if slots:
                    self.ring_ready = [sem(f"ring_ready_{name}{n}") for n in range(slots)]
                    self.u_staged = one("u_staged")
                    self.dense_done = one("dense_done")
                    self.acc_done = one("acc_done")
                    self.sum_copied = one("sum_copied")
                    self.turned = one("turned")
                    self.out_turned = one("out_turned")
                    self.dense_stored = one("dense_stored")
                    self.dense_loaded = one("dense_loaded")

        S_DENSE = EdgeSems("dense", len(FAST_PARTS), SLOTS)
        S_ALL = EdgeSems("all", len(ALL_PARTS))
        S_ATT = EdgeSems("att", 1)
        x1_staged = sem("x1_staged")
        x1T_done = sem("x1T_done")
        x1T_copied = sem("x1T_copied")
        kvq_done = sem("kvq_done")
        kvq_copied = sem("kvq_copied")
        kvq_stored = [sem("kvq_stored0"), sem("kvq_stored1")]
        q_cleared = sem("q_cleared")
        q_scattered = [sem("q_scattered0"), sem("q_scattered1")]
        q_scanned = sem("q_scanned")
        ones_row = sem("ones_row")
        attr_loaded = [sem("attr_loaded0"), sem("attr_loaded1")]
        attrT_done = sem("attrT_done")
        attrT_copied = sem("attrT_copied")
        eproj_done = sem("eproj_done")
        clipped = sem("clipped")
        exp_done = sem("exp_done")
        kv_used = sem("kv_used")
        y_done = sem("y_done")
        y_stored = sem("y_stored")
        blank_ready = sem("blank_ready")
        passed = sem("passed")

        def wait_count(eng, sem, count):
            eng.wait_ge(sem, count)
            eng.sem_inc(passed, 1)

        FREE_G = 2 * CG
        FREE_F = 2
        FREE_R = SLOTS
        FREE_B = 2

        PG = 2 * CG

        def att_group(i, idx):
            idx_pair, in_pair = idx // PG, idx % PG
            return (i + idx_pair if idx_pair else i), in_pair // CG, in_pair % CG

        def att_pairs(eng, pair):
            pair(0, True, False)
            with eng.Fori(1, PAIRS - 1) as i:
                pair(i, False, False)
            pair(PAIRS - 1, False, True)

        block = ctx.enter_context(nc.Block())

        def choose(eng):
            way = eng.alloc_register(f"way_{eng.engine.name}")
            eng.wait_ge(flag_ready, 1)
            eng.reg_load(way, flag[0:1, 0:1])
            return way

        @block.sync
        def _(sp):
            sp.wait_ge(cleared, 1)
            for a, nat in ((src, src_nat), (dst, dst_nat), (edge_weight, w_nat)):
                full = (QB - 1) * P
                sp.dma_start(nat[:, 0:QB - 1, :], a[0:full * GE].rearrange("(r p i) -> p r i", p=P, i=GE)).then_inc(loaded_e, 16)
                sp.dma_start(nat[0:QF - full, QB - 1, :], a[full * GE:QF * GE].rearrange("(p i) -> p i", i=GE)).then_inc(loaded_e, 16)
                sp.dma_start(nat[QF - full:QF - full + 1, QB - 1, 0:REST], a[QF * GE:E].rearrange("(p i) -> p i", p=1)).then_inc(loaded_e, 16)
            full = (QB - 1) * P
            sp.dma_start(prev_nat[0:1, 0, 1:GE], dst[0:GE - 1].rearrange("(p i) -> p i", p=1)).then_inc(loaded_e, 16)
            sp.dma_start(prev_nat[1:P, 0, :], dst[GE - 1:P * GE - 1].rearrange("(p i) -> p i", i=GE)).then_inc(loaded_e, 16)
            sp.dma_start(prev_nat[:, 1:QB - 1, :], dst[P * GE - 1:full * GE - 1].rearrange("(r p i) -> p r i", p=P, i=GE)).then_inc(loaded_e, 16)
            sp.dma_start(prev_nat[0:QF - full, QB - 1, :], dst[full * GE - 1:QF * GE - 1].rearrange("(p i) -> p i", i=GE)).then_inc(loaded_e, 16)
            sp.dma_start(prev_nat[QF - full:QF - full + 1, QB - 1, 0:REST], dst[QF * GE - 1:E - 1].rearrange("(p i) -> p i", p=1)).then_inc(loaded_e, 16)
            sp.dma_start(far_nat[:, 0, :], dst[FAR * GE:(FAR + P) * GE].rearrange("(p i) -> p i", i=GE)).then_inc(loaded_e, 16)
            sp.dma_start(far_nat[0:DQ - FAR - P, 1, :], dst[(FAR + P) * GE:DE].rearrange("(p i) -> p i", i=GE)).then_inc(loaded_e, 16)
            sp.dma_start(w_kvq[0:D, 0:D], WK).then_inc(loaded_w, 16)
            sp.dma_start(w_kvq[0:D, D:2 * D], WV).then_inc(loaded_w, 16)
            sp.dma_start(w_kvq[0:D, 2 * D:3 * D], WQ).then_inc(loaded_w, 16)
            sp.dma_start(w_e[0:D, :], WE).then_inc(loaded_w, 16)
            for b, to in ((bK, w_kvq[D:D + 1, 0:D]), (bV, w_kvq[D:D + 1, D:2 * D]), (bQ, w_kvq[D:D + 1, 2 * D:3 * D]), (bE, w_e[D:D + 1, :])):
                sp.dma_start(to, b.rearrange("(p f) -> p f", p=1)).then_inc(loaded_w, 16)
            sp.wait_ge(same_nat_ready, 1)
            full = (QB - 1) * P
            sp.dma_start(same_rows[0:full * GE].rearrange("(r p i) -> p r i", p=P, i=GE), same_nat[:, 0:QB - 1, :]).then_inc(same_stored, 16)
            sp.dma_start(same_rows[full * GE:NQ * GE].rearrange("(p i) -> p i", i=GE), same_nat[0:NQ - full, QB - 1, :]).then_inc(same_stored, 16)
            sp.wait_ge(blank_ready, 1)
            DZ = 20
            for j0 in range(0, NJ, DZ):
                sp.dma_start(dense_v[:, j0:j0 + DZ, :].rearrange("p j (s c) -> p (j s) c", s=2),
                             blank.unsqueeze(1).broadcast_to([P, 2 * DZ, DENSE_PITCH // 2])).then_inc(dense_cleared, 16)
            sp.wait_ge(cleared, 2)
            for p0, p1 in ((0, 112), (112, NP)):
                sp.dma_start(x_sb[p0:p1, :], x[p0 * NJ:p1 * NJ, :].rearrange("(p j) f -> p (j f)", j=NJ)).then_inc(loaded_x, 16)
            sp.wait_ge(nat_T_all, 1)
            def by_stream(of):
                return of[0:DE].rearrange("(s r e) -> s r e", s=STREAMS, e=GE)

            with sp.Fori(0, F_PAIR) as i:
                for m in range(2):
                    for b in range(2):
                        sp.wait_ge(row_used, (i * 2 + m) * 2 + b + 1)
                        for a, of in enumerate((src, dst, edge_weight)):
                            for n in range(2):
                                to = row_in[:, b, a, n * GE:(n + 1) * GE]
                                sp.dma_start(to if a == 2 else to.bitcast(I32),
                                             by_stream(of)[b * 2 + n, bass.ds(i * 2 + m, 1), :].rearrange("r e -> (r e)").partition_broadcast(P)).then_inc(row_loaded[b], 16)

            def zero_ends(S, F):
                rows, half = sum_rows(F), P // 2
                end = rows.shape[0] - P
                for b in range(2):
                    sp.dma_start(rows[end + b * half:end + (b + 1) * half, :], zeros[0:half, 0:D]).then_inc(S.rows_stored[b], 16)

            def load_same(S, b, at):
                rows = P if S is S_ATT else D
                sp.dma_start(same[0:rows, b, :], same_rows[at].partition_broadcast(rows)).then_inc(S.same_ready[b], 16)

            def edge_chunk(S, F, q, i, b):
                c = q * 2 + b
                sp.wait_ge(S.scan_done, c * CG + CG + FREE_F)
                load_same(S, b, bass.ds(i * (2 * CE) + (2 * F + b + 2) * CE, CE))
                sp.wait_ge(S.out_copied, c * CG + CG + FREE_B)
                sp.dma_start(by_group(sum_rows(F))[:, bass.ds(i * (2 * CG) + b * CG, CG), :],
                             rows_out[:, b, :, :].rearrange("p (g u) f -> p g (u f)", u=GT)).then_inc(S.rows_stored[b], 16)

            def load_unit(S, k, i, n):
                half, jj = n // UNIT_J, n % UNIT_J
                sp.wait_ge(S.dense_done, (k * D_ITERS + i) * (2 * UNIT_J) + n + 1)
                col = dense_v[:, bass.ds(i * UNIT_J + jj, 1), 0:DN].rearrange("p j (t s c) -> p j t s c", t=2, s=2)[:, 0, :, half, :]
                sp.dma_start(ring[:, jj, :, :], col).then_inc(S.ring_ready[jj], 16)

            def first_marks(S, F):
                sp.dma_start(same_rows[NQ * GE:(NQ + WRAP) * GE].rearrange("(p i) -> p i", i=GE),
                             same_rows[F * 2 * CE:(F + 1) * 2 * CE].rearrange("(p i) -> p i", i=GE)).then_inc(S.restarted, 16)
                sp.wait_ge(S.restarted, 16)
                sp.dma_start(same_rows[NQ * GE:NQ * GE + 1].rearrange("(p i) -> p i", i=1), zeros[0:1, 0:1].bitcast(BF16)[:, 0:1]).then_inc(S.restarted, 16)
                sp.wait_ge(S.restarted, 32)
                for b in range(2):
                    load_same(S, b, slice((NQ + b * CG) * GE, (NQ + (b + 1) * CG) * GE))

            def store_steps(S, F, parts, dense_way):
                n_pairs = PAIRS - F
                first_marks(S, F)
                if dense_way:
                    for st in range(STREAMS):
                        sp.wait_ge(added[st], RG * GT * 16)
                zero_ends(S, F)
                sp.wait_ge(node_init, 1)
                sp.dma_start(node_rows_v, u_sb[:, :]).then_inc(S.node_stored, 16)
                for k0, n_steps in parts:
                    with sp.Fori(0, n_steps) as kk:
                        k = kk + k0
                        if dense_way:
                            def pair(i, ahead):
                                for b in range(2):
                                    for n in range(UNIT_J):
                                        if b == 0:
                                            load_unit(S, k, i, UNIT_J + n)
                                        elif ahead:
                                            load_unit(S, k, i + 1, n)
                                    edge_chunk(S, F, k * n_pairs + i, i, b)
                            for n in range(UNIT_J):
                                load_unit(S, k, 0, n)
                            with sp.Fori(0, D_ITERS - 1) as i:
                                pair(i, True)
                            pair(D_ITERS - 1, False)
                            sp.wait_ge(S.out_turned, (k + 1) * TURNS + 1)
                            for t in range(2):
                                sp.dma_start(dense_rows[t * DN // 2:(t + 1) * DN // 2, :].rearrange("(a j) f -> j a f", j=NJ),
                                             dense_out[0:NJ, :, t, :]).then_inc(S.dense_stored, 16)
                            sp.wait_ge(S.dense_stored, (k + 1) * 32)
                            sp.dma_start(dense_n[0:NODE_DENSE, :], dense_rows.rearrange("(p j) f -> p (j f)", j=NJ)).then_inc(S.dense_loaded, 16)
                            with sp.Fori(D_ITERS, n_pairs) as i:
                                for b in range(2):
                                    edge_chunk(S, F, k * n_pairs + i, i, b)
                        else:
                            with sp.Fori(0, n_pairs) as i:
                                for b in range(2):
                                    edge_chunk(S, F, k * n_pairs + i, i, b)
                        with sp.Fori(0, NODE_PAIRS) as j:
                            for b in range(2):
                                n = (k * NODE_PAIRS + j) * 2 + b
                                sp.wait_ge(S.node_done, n + 1 + 2)
                                cols = bass.ds((j * 2 + b) * (NB * D), NB * D)
                                sp.dma_start(node_rows_v[:, cols], u_sb[:, cols]).then_inc(S.node_stored, 16)
                for b in range(2):
                    sp.wait_ge(S.same_ready[b], 16 * (1 + STEPS * n_pairs))

            way = choose(sp)
            with sp.If_eq(way, 0):
                store_steps(S_DENSE, F_PAIR, FAST_PARTS, True)
            with sp.Else():
                store_steps(S_ALL, 0, ALL_PARTS, False)

            with sp.Fori(0, NODE_PAIRS) as j:
                for b in range(2):
                    n = j * 2 + b
                    sp.wait_ge(kvq_copied, n + 1)
                    sp.dma_start(kv_rows_v[:, bass.ds(n * NB, NB), :], kvq_out[:, b, :, 0:2 * D]).then_inc(kvq_stored[b], 16)
            for b in range(2):
                sp.wait_ge(kvq_stored[b], 16 * NODE_PAIRS)
                sp.wait_ge(q_scattered[b], 16 * NB * NODE_PAIRS)
            sp.wait_ge(attr_copied, 16 * (2 + (EP - E) // 64))
            for b in range(2):
                load_same(S_ATT, b, slice(b * CE, (b + 1) * CE))
            zero_ends(S_ATT, 0)

            def load_attr(b, at):
                for grp in range(CG):
                    for a, of in enumerate((attr_rows_v, q_starts_v)):
                        sp.dma_start(attr_in[:, b, grp * GT:(grp + 1) * GT, a * D:(a + 1) * D],
                                     of[:, at(grp), :, :].rearrange("p g u f -> p (g u) f")).then_inc(attr_loaded[b], 16)

            for b in range(2):
                load_attr(b, lambda grp: slice(b * CG + grp, b * CG + grp + 1))

            def attr_load(i, b):
                sp.wait_ge(attrT_done, (i * 2 + b + 1) * CG + 2)
                load_attr(b, lambda grp: bass.ds(i * (2 * CG) + (b + 2) * CG + grp, 1))

            with sp.Fori(0, PAIRS - 1) as i:
                for b in range(2):
                    attr_load(i, b)
                    edge_chunk(S_ATT, 0, i, i, b)
            for b in range(2):
                edge_chunk(S_ATT, 0, PAIRS - 1, PAIRS - 1, b)
            sp.wait_ge(y_done, 1)
            for p0, p1 in ((0, 112), (112, NP)):
                sp.dma_start(out[p0 * NJ:p1 * NJ, :].rearrange("(p j) f -> p (j f)", j=NJ), h_sb[p0:p1, :]).then_inc(y_stored, 16)
            sp.wait_ge(y_stored, 32)
            for b in range(2):
                sp.wait_ge(S_ATT.same_ready[b], 16 * (1 + PAIRS))

        @block.gpsimd
        def _(pool):
            g = nc.gpsimd
            pool.memset(zeros[:, :], 0.0).then_inc(consts, 1)
            pool.memset(ident[:, :], 0.0)
            pool.memset(lower[:, :], 1.0)
            pool.memset(earlier[:, :], 1.0)
            pool.iota(iota_p[:, :], pattern=[[1, P]], base=0, channel_multiplier=0, allow_small_or_imprecise_dtypes=True)
            pool.iota(iota_j[:, :], pattern=[[1, NJ]], base=0, channel_multiplier=0, allow_small_or_imprecise_dtypes=True)
            pool.iota(no_edges[:, :], pattern=[[1, NJ]], base=EP, channel_multiplier=NJ, allow_small_or_imprecise_dtypes=True)
            pool.memset(ones[:, :], 1.0).then_inc(consts, 1)
            pool.wait_ge(consts, 2)
            pool.affine_select(out=ident[:, :], in_=ident[:, :], compare_op=ALU.not_equal, fill=1.0, base=0,
                               pattern=[[-1, P]], channel_multiplier=1)
            pool.affine_select(out=lower[:, :], in_=lower[:, :], compare_op=ALU.is_gt, fill=0.0, base=0,
                               pattern=[[1, P]], channel_multiplier=-1)
            pool.affine_select(out=earlier[:, :], in_=earlier[:, :], compare_op=ALU.is_gt, fill=0.0, base=0,
                               pattern=[[-1, P]], channel_multiplier=1).then_inc(consts, 1)

            pool.wait_ge(dense_cleared, 16 * 5)
            def add_groups(i, m, at_start=False):
                grp = i * 2 + m
                wait_count(pool, add_ready, grp * 2 + 2)
                for u in range(GT):
                    for st in range(STREAMS):
                        if not (at_start and u == 0):
                            wait_count(pool, added[st], grp * (GT * 16) + u * 16)
                        g.indirect_dma_start(out=dense, out_offset=bass.IndirectOffsetOnAxis(ap=add_idx[:, m, st, u:u + 1].bitcast(U32), axis=0),
                                             in_=add_w[:, m, st, u:u + 1], in_offset=None, compute_op=ALU.add).then_inc(added[st], 16)
                    if u == 0 and not at_start:
                        pool.sem_inc(add_used, 1)

            add_groups(0, 0, at_start=True)
            add_groups(0, 1)
            with pool.Fori(1, F_PAIR) as i:
                for m in range(2):
                    add_groups(i, m)
            for st in range(STREAMS):
                pool.wait_ge(added[st], RG * GT * 16)

            def gather_ends(S, k, F):
                for b in range(2):
                    wait_count(pool, S.rows_stored[b], (k + 1) * (16 * (PAIRS - F)) + 16)
                with pool.Fori(0, NODE_PAIRS) as j:
                    for b in range(2):
                        n = (k * NODE_PAIRS + j) * 2 + b
                        wait_count(pool, S.end_staged, n + 1)
                        wait_count(pool, S.node_done, n + 1)
                        for t in range(NB):
                            g.indirect_dma_start(out=ends_in[:, b, t, :], out_offset=None, in_=sum_rows(F),
                                                 in_offset=bass.IndirectOffsetOnAxis(ap=end_st[:, b, t:t + 1].bitcast(U32), axis=0)).then_inc(S.ends_gathered[b], 16)

            def gather_steps(S, F, parts):
                n_pairs = PAIRS - F
                for part, (k0, n_steps) in enumerate(parts):
                    with pool.Fori(0, n_steps) as kk:
                        k = kk + k0
                        wait_count(pool, S.node_stored, k * (16 * NODE_BLOCKS) + 16)
                        with pool.Fori(0, n_pairs) as i:
                            for b in range(2):
                                c = (k * n_pairs + i) * 2 + b
                                wait_count(pool, S.staged, c + 1)
                                wait_count(pool, S.scaled_done, c * CG + CG)
                                for t in range(CT):
                                    g.indirect_dma_start(out=rows_in[:, b, t, :], out_offset=None, in_=node_rows,
                                                         in_offset=bass.IndirectOffsetOnAxis(ap=src_st[:, b, t:t + 1].bitcast(U32), axis=0)).then_inc(S.gathered[part][b], 16)
                        gather_ends(S, k, F)

            way = choose(pool)
            with pool.If_eq(way, 0):
                gather_steps(S_DENSE, F_PAIR, FAST_PARTS)
            with pool.Else():
                gather_steps(S_ALL, 0, ALL_PARTS)

            pool.wait_ge(q_cleared, 16 * 4)
            with pool.Fori(0, NODE_PAIRS) as j:
                for b in range(2):
                    wait_count(pool, kvq_copied, j * 2 + b + 1)
                    for t in range(NB):
                        g.indirect_dma_start(out=q_starts, out_offset=bass.IndirectOffsetOnAxis(ap=start_st[:, b, t:t + 1].bitcast(U32), axis=0),
                                             in_=kvq_out[:, b, t, 2 * D:3 * D], in_offset=None).then_inc(q_scattered[b], 16)
            for b in range(2):
                pool.wait_ge(kvq_stored[b], 16 * NODE_PAIRS)
            with pool.Fori(0, PAIRS) as i:
                for b in range(2):
                    c = i * 2 + b
                    wait_count(pool, S_ATT.staged, c + 1)
                    wait_count(pool, kv_used, (c + 1) * CG)
                    for t in range(CT):
                        g.indirect_dma_start(out=kv_in[:, b, t, :], out_offset=None, in_=kv_rows,
                                             in_offset=bass.IndirectOffsetOnAxis(ap=src_st[:, b, t:t + 1].bitcast(U32), axis=0)).then_inc(S_ATT.gathered[0][b], 16)
            gather_ends(S_ATT, 0, 0)

        @block.scalar
        def _(act):
            act.wait_ge(nat_ready, 1)
            act.wait_ge(consts, 1)
            half = E // 32 * 16
            act.dma_start(attr_rows[0:half, :].rearrange("(a b) f -> a (b f)", a=16), edge_attr[0:half, :].rearrange("(a b) f -> a (b f)", a=16)).then_inc(attr_copied, 16)
            act.dma_start(attr_rows[half:E, :].rearrange("(a b) f -> a (b f)", a=16), edge_attr[half:E, :].rearrange("(a b) f -> a (b f)", a=16)).then_inc(attr_copied, 16)
            for r0 in range(E, EP, 64):
                act.dma_start(attr_rows[r0:r0 + 64, :], zeros[0:64, 0:D]).then_inc(attr_copied, 16)
            size = (EP + NT) * D // (4 * P)
            flat = q_starts.rearrange("(a p r) f -> a p (r f)", a=4, p=P)
            for a in range(4):
                act.dma_start(flat[a].rearrange("p (s c) -> p s c", c=3 * D), zeros[:, 0:3 * D].unsqueeze(1).broadcast_to([P, size // (3 * D), 3 * D])).then_inc(q_cleared, 16)
            with act.Fori(0, HOT_ITERS) as i:
                for n in range(8):
                    act.wait_ge(hots_plain, i * 8 + n + 1)
                    for t in range(HB):
                        o = hots[:, n % 2, t, :]
                        w_col = w_p[:, bass.ds(i * (8 * HB) + (n * HB + t), 1)]
                        nc.scalar.activation(o[:, P:P + NJ], o[:, P + NJ:P + 2 * NJ], ACT.Copy, scale=w_col)
                        last = nc.scalar.activation(o[:, 2 * P + 2 * NJ:HOT], o[:, 2 * P + 2 * NJ:HOT], ACT.Copy, scale=w_col)
                    last.then_inc(hots_ready, 1)
            act.wait_ge(root_in, 1)
            nc.scalar.activation(deg_t[:, 0:2, :], deg[:, 0:2, :], ACT.Sqrt).then_inc(root_done, 1)

            def copy_out(S, q, b, g):
                G = (q * 2 + b) * CG + g
                act.wait_ge(S.back_done, G + 1 + FREE_G)
                nc.scalar.activation(rows_out[:, b, g * GT:(g + 1) * GT, :], back[:, g % 2, 0:GT * D].rearrange("p (t f) -> p t f", f=D), ACT.Copy).then_inc(S.out_copied, 1)

            def scale_steps(S, F, parts, dense_way):
                n_pairs = PAIRS - F
                act.sem_inc(S.scaled_done, FREE_G)
                act.sem_inc(S.out_copied, FREE_B)
                if dense_way:
                    act.sem_inc(S.out_turned, 1)
                for part, (k0, n_steps) in enumerate(parts):
                    with act.Fori(0, n_steps) as kk:
                        k = kk + k0

                        def pair(i, with_dense):
                            q = k * n_pairs + i
                            if with_dense:
                                act.wait_ge(S.dense_done, (k * D_ITERS + i) * (2 * UNIT_J) + FREE_R)
                                nc.scalar.activation(u_st[:, :], u_sb[:, bass.ds(i * (UNIT_J * D), UNIT_J * D)], ACT.Copy).then_inc(S.u_staged, 1)
                            for b in range(2):
                                act.wait_ge(S.gathered[part][b], (kk * n_pairs + i + 1) * (16 * CT))
                                act.wait_ge(S.fwd_done, (q * 2 + b) * CG + CG)
                                for g in range(CG):
                                    for t in range(g * GT, (g + 1) * GT):
                                        last = nc.scalar.activation(scaled[:, b, t, :], rows_in[:, b, t, :], ACT.Copy, scale=w_st[:, b, t:t + 1])
                                    last.then_inc(S.scaled_done, 1)
                                act.wait_ge(S.rows_stored[b], q * 16 + 16)
                                for g in range(CG):
                                    copy_out(S, q, b, g)

                        if dense_way:
                            wait_count(act, S.node_done, k * NODE_BLOCKS + 2)
                            with act.Fori(0, D_ITERS) as i:
                                pair(i, True)
                            act.wait_ge(S.acc_done, k + 1)
                            nc.scalar.activation(dense_sum.rearrange("p (b c) -> p b c", b=4), fwd[:, :, 0:DC], ACT.Copy).then_inc(S.sum_copied, 1)
                            for r in range(TURNS):
                                turn = min(4, HALF_P - r * 4)
                                act.wait_ge(S.turned, k * TURNS + r + 1)
                                nc.scalar.activation(dense_out[0:NJ, r * 4:r * 4 + turn, :, :].rearrange("p a t f -> p (a t f)"), fwd[0:NJ, r % 4, 0:turn * P], ACT.Copy).then_inc(S.out_turned, 1)
                            with act.Fori(D_ITERS, n_pairs) as i:
                                pair(i, False)
                        else:
                            with act.Fori(0, n_pairs) as i:
                                pair(i, False)

            way = choose(act)
            with act.If_eq(way, 0):
                scale_steps(S_DENSE, F_PAIR, FAST_PARTS, True)
            with act.Else():
                scale_steps(S_ALL, 0, ALL_PARTS, False)
            act.wait_ge(root_in, 2)
            nc.scalar.activation(stat[:, 0, :], stat[:, 1, :], ACT.Sqrt).then_inc(root_done, 1)
            with act.Fori(0, NODE_PAIRS) as j:
                for b in range(2):
                    n = j * 2 + b
                    act.wait_ge(x1T_done, n + 1)
                    act.wait_ge(kvq_done, n + 1)
                    nc.scalar.activation(xT[0:D, b, :, :].rearrange("p j n -> p (j n)"), x1T_ps[0:D, 0:NB * P], ACT.Copy).then_inc(x1T_copied, 1)

            def attr_copy(q, b, g):
                G = (q * 2 + b) * CG + g
                act.wait_ge(attrT_done, G + 1 + 2)
                act.wait_ge(eproj_done, G + 1)
                nc.scalar.activation(attrT[0:D, g % 2, :].rearrange("p (u e) -> p u e", u=GT),
                                     fwd[0:D, g % 2, :].rearrange("p (e u) -> p u e", u=GT), ACT.Copy).then_inc(attrT_copied, 1)

            def copy_att(q, b, g):
                if g == 0:
                    act.wait_ge(S_ATT.rows_stored[b], q * 16 + 16)
                copy_out(S_ATT, q, b, g)

            def att_scores(i, first, last):
                for g in range(PG):
                    act.wait_ge(clipped, i * PG + g + 1)
                    nc.scalar.activation(score[:, g % 2, :, :], score[:, g % 2, :, :], ACT.Exp).then_inc(exp_done, 1)
                    if not (first and g < 2):
                        copy_att(*att_group(i, g - 2))
                    if not (last and g + 2 >= PG):
                        attr_copy(*att_group(i, g + 2))

            act.sem_inc(S_ATT.out_copied, FREE_B)
            for g in range(2):
                attr_copy(0, 0, g)
            att_pairs(act, att_scores)
            for g in range(2):
                copy_att(*att_group(PAIRS, g - 2))
            act.wait_ge(root_in, 3)
            nc.scalar.activation(stat[:, 0, :], stat[:, 1, :], ACT.Sqrt).then_inc(root_done, 1)

        @block.vector
        def _(dve):
            v = nc.vector
            link = Chain(dve, vec_pre)
            dve.sem_inc(row_used, 2)
            v.memset(blank, 0.0).then_inc(blank_ready, 1)
            v.memset(dst_nat[:, QB - 1, :], NT)
            v.memset(src_nat[:, QB - 1, :], 0)
            v.memset(w_nat[:, QB - 1, :], 0.0)
            v.memset(prev_nat[:, QB - 1, :], 0)
            v.memset(h_sb[:, :], 0.0)
            link(v.memset(prev_nat[0:1, 0, 0:1], -1))
            v.memset(sums[:, 1, :], 0.0).then_inc(cleared, 1)
            dve.wait_ge(loaded_e, 16 * 16)
            v.tensor_copy(dst_f, dst_nat)
            v.tensor_copy(prev_f, prev_nat)
            link(v.tensor_copy(src_f, src_nat))
            dve.sem_inc(nat_ready, 1)
            v.tensor_tensor(same_nat, dst_f, prev_f, ALU.is_equal).then_inc(same_nat_ready, 1)
            DR = DQ - P
            v.memset(bad[:, :], 0.0)
            link(v.tensor_scalar(src_nf, dst_f, float(DN), None, ALU.is_ge))
            link(v.tensor_reduce(bad[:, 0:1], src_nf[:, 0, :], AX, ALU.add))
            link(v.tensor_reduce(bad[0:DR, 1:2], src_nf[0:DR, 1, :], AX, ALU.add))
            FR = DQ - FAR - P
            v.tensor_tensor(far_eq[:, 0, :], dst_f[:, 0, :], far_nat[:, 0, :], ALU.is_equal)
            link(v.tensor_tensor(far_eq[0:FR, 1, :], dst_f[0:FR, 1, :], far_nat[0:FR, 1, :], ALU.is_equal))
            v.tensor_reduce(bad[:, 2:3], far_eq[:, 0, :], AX, ALU.add)
            link(v.tensor_reduce(bad[0:FR, 3:4], far_eq[0:FR, 1, :], AX, ALU.add))
            link(v.tensor_reduce(bad[:, 0:1], bad[:, :], AX, ALU.add))
            dve.sem_inc(bad_ready, 1)
            dve.wait_ge(bad_summed, 1)
            v.tensor_scalar(flag[:, :], back[0:1, 0, 0:1], 0.0, None, ALU.is_gt).then_inc(flag_ready, 1)
            n = 0
            for a, to in ((0, src_pf), (1, dst_pf), (2, w_p[:, 0:NT_TILES])):
                to_v = to.rearrange("p (q u) -> p u q", u=GT)
                for r in range(QB):
                    rows = min(P, NQ - r * P)
                    dve.wait_ge(nat_T, n + 1)
                    link(v.tensor_copy(to_v[:, :, r * P:r * P + rows], fwd[:, n % 4, :].rearrange("p (u q) -> p u q", u=GT)[:, :, 0:rows]))
                    dve.sem_inc(nat_T_used, 1)
                    n += 1
            v.tensor_copy(src_idx[:, 0:NT_TILES], src_pf)
            link(v.tensor_scalar(dst_idx[:, 0:NT_TILES], dst_pf, float(NT - 1), None, ALU.min))
            dve.sem_inc(nat_T_all, 1)
            link(v.tensor_scalar(dense_idx[:, :], src_idx[:, 0:DT], DENSE_PITCH.bit_length() - 1, None, ALU.logical_shift_left))
            link(v.tensor_tensor(dense_idx[:, :], dense_idx[:, :], dst_idx[:, 0:DT], ALU.bitwise_or))
            dve.sem_inc(add_used, 2)
            for f, hi, lo in ((src_pf, src_hi, src_lo), (dst_pf, dst_hi, dst_lo)):
                link(v.tensor_scalar(hi, f, 1.0 / NJ, 0.5 / NJ - 0.5, ALU.mult, ALU.add))
                link(v.tensor_scalar(hi, hi, ROUND, None, ALU.add))
                link(v.tensor_scalar(hi, hi, ROUND, None, ALU.subtract))
                link(v.scalar_tensor_tensor(lo, hi, -float(NJ), f, ALU.mult, ALU.add))
            dve.wait_ge(same_stored, 32)
            link(v.memset(x_sb[96:P, :], 0.0))
            dve.sem_inc(cleared, 1)
            def add_half(i, m, b):
                grp = i * 2 + m
                chain = Chain(dve, vec_add, (grp * 2 + b) * 5)
                dve.wait_ge(row_loaded[b], grp * (6 * 16) + 6 * 16)
                two = slice(b * 2, b * 2 + 2)

                def row(a, t):
                    z = row_in[:, b, a, :].rearrange("p (g e u) -> p g u e", g=2, u=GT)[:, t // GT, t % GT, :]
                    return z if a == 2 else z.bitcast(I32)

                def col(of, t):
                    return of[:, bass.ds(i * (2 * GT) + (((b * 2 + t // GT) * RG + m) * GT + t % GT), 1)]

                for t in range(8):
                    last = v.tensor_scalar(eq_src[:, t, :], row(0, t), col(src_pf, t), None, ALU.is_equal)
                chain(last)
                for t in range(8):
                    last = v.scalar_tensor_tensor(eq_both[:, t, :], row(1, t), col(dst_pf, t), eq_src[:, t, :], ALU.is_equal, ALU.mult)
                chain(last)
                dve.wait_ge(add_used, grp + 1)
                for t in range(8):
                    v.tensor_tensor_reduce(out=eq_junk[:, t, :], in0=eq_both[:, t, :], in1=row(2, t), scale=1.0, scalar=0.0,
                                           op0=ALU.mult, op1=ALU.add, accum_out=add_w[:, m, b * 2 + t // GT, t % GT:t % GT + 1])
                    last = v.tensor_tensor_reduce(out=eq_src[:, t, :], in0=eq_both[:, t, :], in1=earlier[:, :], scale=1.0, scalar=0.0,
                                                  op0=ALU.mult, op1=ALU.add, accum_out=repeats[:, t:t + 1])
                chain(last)
                dve.sem_inc(row_used, 1)
                chain(v.tensor_scalar(add_idx[:, m, two, :], repeats[:, :].rearrange("p (s u) -> p s u", u=GT), 0.0, float(DENSE_PITCH - 1), ALU.is_gt, ALU.mult))
                chain(v.tensor_tensor(add_idx[:, m, two, :], add_idx[:, m, two, :],
                                      dense_idx[:, :].rearrange("p (s t) -> p s t", s=STREAMS)[:, two, bass.ds(i * (2 * GT) + m * GT, GT)], ALU.bitwise_or))
                dve.sem_inc(add_ready, 1)

            def one_hots(i, n):
                dve.wait_ge(hots_used, i * 8 + n + 1)
                at = bass.ds(i * (8 * HB) + n * HB, HB)
                for digit, c, size, iota in ((dst_lo, P + NJ, NJ, iota_j), (src_lo, 2 * P + 2 * NJ, NJ, iota_j),
                                             (dst_hi, 0, P, iota_p), (src_hi, P + 2 * NJ, P, iota_p)):
                    last = v.tensor_tensor(hots[:, n % 2, :, c:c + size], iota[:, 0:size].unsqueeze(1).broadcast_to([P, HB, size]),
                                           digit[:, at].unsqueeze(2).broadcast_to([P, HB, size]), ALU.is_equal)
                last.then_inc(hots_plain, 1)

            assert HOT_ITERS * 8 * HB == NT_TILES and HOT_ITERS > F_PAIR
            ahead = HOT_ITERS - F_PAIR
            with dve.Fori(0, ahead) as i:
                for n in range(8):
                    one_hots(i, n)
            with dve.Fori(0, F_PAIR) as i:
                for m in range(2):
                    for b in range(2):
                        add_half(i, m, b)
                        for n in range(2):
                            one_hots(i + ahead, m * 4 + b * 2 + n)
            dve.wait_ge(counted, 1)
            v.tensor_scalar(deg[:, 1, :], back[:, 0, 0:NJ], 1.0, None, ALU.add)
            v.tensor_copy(count[:, :], back[:, 0, NJ:2 * NJ])
            link(v.tensor_scalar(deg[:, 0, :], back[:, 1, 0:NJ], 1.0, None, ALU.add))
            v.tensor_scalar(inv_out[:, :], deg[:, 0, :], 0.0, None, ALU.is_gt)
            link(v.tensor_scalar(inv_in9[:, :], deg[:, 1, :], 0.0, 1.0 - ALPHA, ALU.is_gt, ALU.mult))
            link(v.tensor_scalar(deg[:, 0:2, :], deg[:, 0:2, :], 1e-30, None, ALU.max))
            dve.sem_inc(root_in, 1)
            dve.wait_ge(root_done, 1)
            r2, t2, d2 = deg_t[:, 0:2, :], stat[:, :, :], deg[:, 0:2, :]
            link(v.reciprocal(r2, r2))
            link(v.tensor_tensor(t2, r2, r2, ALU.mult))
            link(v.tensor_tensor(t2, t2, d2, ALU.mult))
            link(v.tensor_scalar(t2, t2, -0.5, 1.5, ALU.mult, ALU.add))
            link(v.tensor_tensor(r2, r2, t2, ALU.mult))
            v.tensor_tensor(inv_out[:, :], inv_out[:, :], deg_t[:, 0, :], ALU.mult)
            v.tensor_tensor(inv_in9[:, :], inv_in9[:, :], deg_t[:, 1, :], ALU.mult)
            link(v.tensor_tensor_scan(deg[:, 2, :], ones[:, :], count[:, :], 0.0, ALU.mult, ALU.add))
            link(v.tensor_copy(first[:, :], deg[:, 2, NJ - 1:NJ]))
            dve.sem_inc(totals_ready, 1)
            dve.wait_ge(offsets_ready, 1)
            link(v.tensor_copy(first[:, :], proj[:, 0, 0:1]))
            link(v.tensor_scalar(deg[:, 2, :], deg[:, 2, :], first[:, 0:1], float(-1 - ZERO_ROW), ALU.add, ALU.add))
            link(v.tensor_scalar(deg_t[:, 2, :], count[:, :], 0.0, None, ALU.is_gt))
            first_e = stat[:, 0, :]
            link(v.tensor_tensor(first_e, deg[:, 2, :], count[:, :], ALU.subtract))
            link(v.tensor_scalar(first_e, first_e, float(1 + ZERO_ROW), None, ALU.add))
            link(v.tensor_tensor(first_e, first_e, no_edges[:, :], ALU.subtract))
            link(v.tensor_tensor(first_e, first_e, deg_t[:, 2, :], ALU.mult))
            link(v.tensor_tensor(start_idx[:, :], first_e, no_edges[:, :], ALU.add))
            link(v.tensor_tensor(deg[:, 2, :], deg[:, 2, :], deg_t[:, 2, :], ALU.mult))
            link(v.tensor_scalar(end_idx[:, 0:NJ], deg[:, 2, :], float(ZERO_ROW), None, ALU.add))
            v.tensor_copy(all_ends[:, :], end_idx[:, 0:NJ])
            link(v.tensor_copy(end_idx[:, NJ:NJ + 2 * NB], end_idx[:, 0:2 * NB]))
            dve.wait_ge(loaded_x, 32)
            link(v.tensor_tensor(u_sb[:, :].rearrange("p (j f) -> p j f", f=D), x_sb[:, :].rearrange("p (j f) -> p j f", f=D),
                                 inv_out[:, :].unsqueeze(2).broadcast_to([P, NJ, D]), ALU.mult))
            dve.sem_inc(node_init, 1)

            def stage(S, b, at):
                v.tensor_copy(src_st[:, b, :], src_idx[:, at])
                v.tensor_copy(w_st[:, b, :], w_p[:, at]).then_inc(S.staged, 1)

            def stage_first(S, F):
                start = Chain(dve, S.vec_first, 6 if F else 0)
                W, f = WRAP * GT, F * 2 * CT
                for a in (src_idx, w_p):
                    last = v.tensor_copy(a[:, NT_TILES:NT_TILES + W], a[:, f:f + W])
                start(last)
                for b in range(2):
                    stage(S, b, slice(f + b * CT, f + (b + 1) * CT))
                    v.tensor_copy(end_st[:, b, :], end_idx[:, b * NB:(b + 1) * NB]).then_inc(S.end_staged, 1)
                dve.sem_inc(S.scan_done, FREE_F)
                dve.sem_inc(S.node_done, 2)

            def scan(S, q, b, g, bank):
                G = (q * 2 + b) * CG + g
                dve.wait_ge(S.fwd_done, G + 1 + FREE_G)
                dve.wait_ge(S.back_done, G + 1)
                if g == 0:
                    dve.wait_ge(S.same_ready[b], (q + 1) * 16)
                    before = sums[0:D, 1 - b, CE - 1:CE]
                else:
                    before = sums[0:D, b, g * GE - 1:g * GE]
                dve.wait_ge(S.scan_done, G + FREE_F)
                v.tensor_tensor_scan(sums[0:D, b, g * GE:(g + 1) * GE], same[0:D, b, g * GE:(g + 1) * GE],
                                     bank, before, ALU.mult, ALU.add).then_inc(S.scan_done, 1)

            def sum_steps(S, F, parts, dense_way):
                n_pairs = PAIRS - F
                per_block = 5 if dense_way else 4
                if dense_way:
                    link = Chain(dve, S.vec_first)
                    end_f, late = deg[:, 2, :], deg_t[:, 2, :]
                    link(v.tensor_copy(end_f, end_idx[:, 0:NJ]))
                    link(v.tensor_scalar(late, end_f, float(DE), None, ALU.is_ge))
                    link(v.tensor_scalar(end_f, end_f, float(-ZERO_ROW), None, ALU.add))
                    link(v.tensor_tensor(end_f, end_f, late, ALU.mult))
                    link(v.tensor_scalar(end_idx[:, 0:NJ], end_f, float(ZERO_ROW - DE), None, ALU.add))
                    link(v.tensor_copy(end_idx[:, NJ:NJ + 2 * NB], end_idx[:, 0:2 * NB]))
                stage_first(S, F)
                for k0, n_steps in parts:
                    final = k0 == STEPS - 1
                    with dve.Fori(0, n_steps) as kk:
                        k = kk + k0
                        with dve.Fori(0, n_pairs) as i:
                            for b in range(2):
                                for g in range(CG):
                                    scan(S, k * n_pairs + i, b, g, proj[0:D, g % 2, :])
                                stage(S, b, bass.ds(i * (2 * CT) + (2 * F + b + 2) * CT, CT))
                        if dense_way:
                            wait_count(dve, S.dense_loaded, k * 16 + 16)
                        with dve.Fori(0, NODE_PAIRS) as j:
                            for b in range(2):
                                blk = k * NODE_PAIRS + j
                                if final:
                                    step = Chain(dve, S.vec_node, (j * 2 + b) * (per_block - 1) + (STEPS - 1) * NODE_BLOCKS * per_block)
                                else:
                                    step = Chain(dve, S.vec_node, (blk * 2 + b) * per_block)
                                dve.wait_ge(S.ends_gathered[b], (blk + 1) * (16 * NB))
                                cols = bass.ds((j * 2 + b) * (NB * D), NB * D)
                                nodes = bass.ds((j * 2 + b) * NB, NB)
                                e3 = ends_in[:, b, :, :]
                                e2 = e3.rearrange("p j f -> p (j f)")
                                step(v.tensor_tensor(e2, e2, u_sb[:, cols], ALU.add))
                                if dense_way:
                                    ed = e2[0:NODE_DENSE]
                                    step(v.tensor_tensor(ed, ed, dense_n[0:NODE_DENSE, cols], ALU.add))
                                step(v.tensor_tensor(e3, e3, inv_in9[:, nodes].unsqueeze(2).broadcast_to([P, NB, D]), ALU.mult))
                                if final:
                                    step(v.scalar_tensor_tensor(u_sb[:, cols], x_sb[:, cols], ALPHA, e2, ALU.mult, ALU.add))
                                else:
                                    step(v.scalar_tensor_tensor(e2, x_sb[:, cols], ALPHA, e2, ALU.mult, ALU.add))
                                    step(v.tensor_tensor(u_sb[:, cols].rearrange("p (j f) -> p j f", f=D), e3, inv_out[:, nodes].unsqueeze(2).broadcast_to([P, NB, D]), ALU.mult))
                                dve.sem_inc(S.node_done, 1)
                                v.tensor_copy(end_st[:, b, :], end_idx[:, bass.ds((j * 2 + b + 2) * NB, NB)]).then_inc(S.end_staged, 1)
                dve.wait_ge(S.node_stored, STEPS * (16 * NODE_BLOCKS) + 16)

            way = choose(dve)
            with dve.If_eq(way, 0):
                sum_steps(S_DENSE, F_PAIR, FAST_PARTS, True)
            with dve.Else():
                sum_steps(S_ALL, 0, ALL_PARTS, False)

            norm = Chain(dve, vec_ln)

            def layernorm(o, s, t, nth):
                s3, t3, o3 = (z[:, :].rearrange("p (j f) -> p j f", f=D) for z in (s, t, o))
                norm(v.tensor_reduce(stat[:, 0, :], s3, AX, ALU.add))
                norm(v.tensor_scalar(stat[:, 0, :], stat[:, 0, :], 1.0 / D, None, ALU.mult))
                norm(v.tensor_tensor(s3, s3, stat[:, 0, :].unsqueeze(2).broadcast_to([P, NJ, D]), ALU.subtract))
                norm(v.tensor_tensor(t3, s3, s3, ALU.mult))
                norm(v.tensor_reduce(stat[:, 1, :], t3, AX, ALU.add))
                norm(v.tensor_scalar(stat[:, 1, :], stat[:, 1, :], 1.0 / D, EPS, ALU.mult, ALU.add))
                dve.sem_inc(root_in, 1)
                dve.wait_ge(root_done, nth)
                norm(v.reciprocal(stat[:, 1, :], stat[:, 0, :]))
                norm(v.tensor_tensor(o3, s3, stat[:, 1, :].unsqueeze(2).broadcast_to([P, NJ, D]), ALU.mult))

            norm(v.tensor_copy(end_idx[:, 0:NJ], all_ends[:, :]))
            norm(v.tensor_copy(end_idx[:, NJ:NJ + 2 * NB], end_idx[:, 0:2 * NB]))
            norm(v.tensor_tensor(h_sb[:, :], u_sb[:, :], x_sb[:, :], ALU.add))
            layernorm(x_sb, h_sb, tmp, 2)
            v.memset(u_sb[D:D + 1, :], 1.0).then_inc(ones_row, 1)

            with dve.Fori(0, NODE_PAIRS) as j:
                for b in range(2):
                    n = j * 2 + b
                    v.tensor_copy(x_st[:, b, :, :].rearrange("p j f -> p (j f)"), x_sb[:, bass.ds(n * (NB * D), NB * D)]).then_inc(x1_staged, 1)
                    dve.wait_ge(kvq_done, n + 1 + 2)
                    for r in range(NB // 2):
                        v.tensor_copy(kvq_out[:, b, 2 * r:2 * r + 2, :].rearrange("p j f -> p (j f)"), kvq_ps(r)[:, 0:2 * 3 * D])
                    v.tensor_copy(start_st[:, b, :], start_idx[:, bass.ds(n * NB, NB)]).then_inc(kvq_copied, 1)
                for b in range(2):
                    dve.wait_ge(kvq_stored[b], (j + 1) * 16)
                    dve.wait_ge(q_scattered[b], (j + 1) * (16 * NB))

            isd = float(1.0 / float(DH) ** 0.5)
            dve.sem_inc(q_scanned, 1)
            stage_first(S_ATT, 0)

            def spread_queries(q, b, g):
                G = (q * 2 + b) * CG + g
                if g == 0:
                    dve.wait_ge(S_ATT.same_ready[b], (q + 1) * 16)
                    before = sums[D:2 * D, 1 - b, CE - 1:CE]
                else:
                    before = sums[D:2 * D, b, g * GE - 1:g * GE]
                dve.wait_ge(attrT_done, G + 1 + 2)
                dve.wait_ge(q_scanned, G + 1)
                v.tensor_tensor_scan(sums[D:2 * D, b, g * GE:(g + 1) * GE], same[D:2 * D, b, g * GE:(g + 1) * GE],
                                     fwd[D:2 * D, g % 2, :], before, ALU.mult, ALU.add).then_inc(q_scanned, 1)

            EC = 6

            def att_messages(i, first, last):
                for n in range(PG):
                    b, g = n // CG, n % CG
                    Gl = i * PG + n
                    if not (last and n + 1 == PG):
                        spread_queries(*att_group(i, n + 1))
                    if g == 0:
                        dve.wait_ge(S_ATT.gathered[0][b], (i + 1) * (16 * CT))
                    edge = Chain(dve, vec_edge, Gl * EC)
                    t0, t1 = g * GT, (g + 1) * GT
                    k4, v4 = kv_in[:, b, t0:t1, 0:D], kv_in[:, b, t0:t1, D:2 * D]
                    q4 = proj[:, g % 2, GT * D:2 * GT * D].rearrange("p (t f) -> p t f", f=D)
                    s4 = score[:, g % 2, :, :]
                    p4 = prod[:, g % 2, :, :]
                    dve.wait_ge(eproj_done, Gl + 1 + 2)
                    edge(v.tensor_tensor(p4, k4, q4, ALU.mult))
                    edge(v.tensor_tensor(p4, p4, proj[:, g % 2, 0:GT * D].rearrange("p (t f) -> p t f", f=D), ALU.mult))
                    edge(v.tensor_reduce(s4, p4.rearrange("p t (h d) -> p t h d", d=DH), AX, ALU.add))
                    edge(v.tensor_scalar(s4, s4, isd, 5.0, ALU.mult, ALU.min))
                    edge(v.tensor_scalar(s4, s4, -5.0, None, ALU.max))
                    dve.sem_inc(clipped, 1)
                    if not (first and n == 0):
                        scan_messages(*att_group(i, n - 1))
                    dve.wait_ge(exp_done, Gl + 1)
                    dve.wait_ge(S_ATT.fwd_done, Gl + FREE_G - 3)
                    edge(v.tensor_tensor(msg[:, g, :, :].rearrange("p t (h d) -> p t h d", d=DH), v4.rearrange("p t (h d) -> p t h d", d=DH),
                                         s4.unsqueeze(3).broadcast_to([P, GT, HEADS, DH]), ALU.mult))
                    dve.sem_inc(kv_used, 1)
                    if g == CG - 1:
                        stage(S_ATT, b, bass.ds(i * (2 * CT) + (b + 2) * CT, CT))

            def scan_messages(q, b, g):
                scan(S_ATT, q, b, g, fwd[0:D, 2 + g % 2, :])

            spread_queries(0, 0, 0)
            att_pairs(dve, att_messages)
            scan_messages(*att_group(PAIRS, -1))
            with dve.Fori(0, NODE_PAIRS) as j:
                for b in range(2):
                    dve.wait_ge(S_ATT.ends_gathered[b], (j + 1) * (16 * NB))
                    cols = bass.ds((j * 2 + b) * (NB * D), NB * D)
                    v.tensor_tensor(h_sb[:, cols], ends_in[:, b, :, :].rearrange("p j f -> p (j f)"), x_sb[:, cols], ALU.add).then_inc(S_ATT.node_done, 1)
                    v.tensor_copy(end_st[:, b, :], end_idx[:, bass.ds((j * 2 + b + 2) * NB, NB)]).then_inc(S_ATT.end_staged, 1)
            dve.wait_ge(S_ATT.node_done, 2 + NODE_BLOCKS)
            layernorm(h_sb, h_sb, tmp, 3)
            dve.sem_inc(y_done, 1)

        @block.tensor
        def _(pe):
            for S in (S_DENSE, S_ALL, S_ATT):
                pe.sem_inc(S.fwd_done, FREE_G)
                pe.sem_inc(S.back_done, FREE_G)
            pe.sem_inc(S_DENSE.dense_done, FREE_R)
            pe.sem_inc(hots_used, 2)
            pe.sem_inc(attrT_done, 2)
            pe.sem_inc(eproj_done, 2)
            pe.sem_inc(kvq_done, 2)
            pe.sem_inc(kv_used, FREE_G)
            pe.wait_ge(consts, 3)
            pe.wait_ge(bad_ready, 1)
            nc.tensor.matmul(back[0:1, 0, 0:1], bad[:, 0:1], ones[:, 0:1], start=True, stop=True).then_inc(bad_summed, 1)
            pe.wait_ge(nat_ready, 1)
            n = 0
            for nat in (src_f, dst_f, w_nat):
                for r in range(QB):
                    rows = min(P, NQ - r * P)
                    if n >= 4:
                        pe.wait_ge(nat_T_used, n - 3)
                    for u in range(GT):
                        last = nc.tensor.transpose(fwd[:, n % 4, u * P:u * P + rows], nat[0:rows, r, u::GT], ident[0:rows, 0:rows])
                    last.then_inc(nat_T, 1)
                    n += 1
            pe.wait_ge(flag_ready, 1)
            nc.tensor.matmul(back[:, 0, 0:2 * NJ], zeros[:, 0:P], zeros[:, 0:2 * NJ], start=True, stop=False)
            nc.tensor.matmul(back[:, 1, 0:NJ], zeros[:, 0:P], zeros[:, 0:NJ], start=True, stop=False)
            with pe.Fori(0, NT_TILES // (2 * HB)) as i:
                for b in range(2):
                    wait_count(pe, hots_ready, i * 2 + b + 1)
                    for t in range(HB):
                        o = hots[:, b, t, :]
                        nc.tensor.matmul(back[:, 0, 0:2 * NJ], o[:, 0:P], o[:, P:P + 2 * NJ], start=False, stop=False)
                        last = nc.tensor.matmul(back[:, 1, 0:NJ], o[:, P + 2 * NJ:2 * P + 2 * NJ], o[:, 2 * P + 2 * NJ:HOT], start=False, stop=False)
                    last.then_inc(hots_used, 1)
            nc.tensor.matmul(back[:, 0, 0:2 * NJ], zeros[:, 0:P], zeros[:, 0:2 * NJ], start=False, stop=True)
            nc.tensor.matmul(back[:, 1, 0:NJ], zeros[:, 0:P], zeros[:, 0:NJ], start=False, stop=True).then_inc(counted, 1)
            pe.wait_ge(totals_ready, 1)
            nc.tensor.matmul(proj[:, 0, 0:1], lower[:, :], first[:, 0:1], start=True, stop=True).then_inc(offsets_ready, 1)

            def turn_back(S, q, b, g):
                G = (q * 2 + b) * CG + g
                wait_count(pe, S.scan_done, G + 1 + FREE_F)
                wait_count(pe, S.out_copied, G + 1)
                for u in range(GT):
                    last = nc.tensor.transpose(back[:, g % 2, u * D:(u + 1) * D], sums[0:D, b, g * GE + u:(g + 1) * GE:GT], ident[0:D, 0:D])
                last.then_inc(S.back_done, 1)

            def clear_sums(first_of, last_of):
                for bank in range(4):
                    for t in range(2):
                        last = nc.tensor.matmul(fwd[t * D:(t + 1) * D, bank, 0:DC], zeros[:, 0:D], zeros[:, 0:DC], start=first_of, stop=last_of, tile_position=(0, t * D))
                return last

            def multiply_unit(S, k, i, n):
                half, jj = n // UNIT_J, n % UNIT_J
                wait_count(pe, S.ring_ready[jj], (k * D_ITERS + i) * 32 + (half + 1) * 16)
                for gg in range(2):
                    for t in range(2):
                        last = nc.tensor.matmul(fwd[t * D:(t + 1) * D, half * 2 + gg, 0:DC], u_st[:, jj * D:(jj + 1) * D],
                                                ring[:, jj, t, gg * DC:(gg + 1) * DC], start=False, stop=False, tile_position=(0, t * D))
                last.then_inc(S.dense_done, 1)

            def turn_steps(S, F, parts, dense_way):
                n_pairs = PAIRS - F
                for k0, n_steps in parts:
                    with pe.Fori(0, n_steps) as kk:
                        k = kk + k0

                        def pair(i, with_dense):
                            q = k * n_pairs + i
                            n = 0
                            if with_dense:
                                wait_count(pe, S.u_staged, k * D_ITERS + i + 1)
                            for b in range(2):
                                for g in range(CG):
                                    G = (q * 2 + b) * CG + g
                                    wait_count(pe, S.scaled_done, G + 1 + FREE_G)
                                    wait_count(pe, S.scan_done, G + 1)
                                    for u in range(GT):
                                        last = nc.tensor.transpose(proj[0:D, g % 2, u::GT], scaled[:, b, g * GT + u, :], ident[:, :])
                                    last.then_inc(S.fwd_done, 1)
                                    if with_dense:
                                        for _ in range(UNIT_J * (g + 1) // CG - UNIT_J * g // CG):
                                            multiply_unit(S, k, i, n)
                                            n += 1
                                    if g > 0:
                                        turn_back(S, q, b, g - 1)
                                turn_back(S, q, b, CG - 1)

                        if dense_way:
                            wait_count(pe, S.out_turned, k * TURNS + 1)
                            clear_sums(True, False)
                            with pe.Fori(0, D_ITERS) as i:
                                pair(i, True)
                            clear_sums(False, True).then_inc(S.acc_done, 1)
                            wait_count(pe, S.sum_copied, k + 1)
                            for r in range(TURNS):
                                if r >= 4:
                                    wait_count(pe, S.out_turned, k * TURNS + r - 2)
                                for a in range(min(4, HALF_P - r * 4)):
                                    at = (r * 4 + a) * NJ
                                    last = nc.tensor.transpose(fwd[0:NJ, r % 4, a * P:(a + 1) * P], dense_sum[:, at:at + NJ], ident[:, :])
                                last.then_inc(S.turned, 1)
                            with pe.Fori(D_ITERS, n_pairs) as i:
                                pair(i, False)
                        else:
                            with pe.Fori(0, n_pairs) as i:
                                pair(i, False)

            way = choose(pe)
            with pe.If_eq(way, 0):
                turn_steps(S_DENSE, F_PAIR, FAST_PARTS, True)
            with pe.Else():
                turn_steps(S_ALL, 0, ALL_PARTS, False)

            pe.wait_ge(loaded_w, 16 * 8)
            pe.wait_ge(ones_row, 1)
            with pe.Fori(0, NODE_PAIRS) as j:
                for b in range(2):
                    n = j * 2 + b
                    wait_count(pe, x1_staged, n + 1)
                    for t in range(NB):
                        last = nc.tensor.transpose(x1T_ps[0:D, t * P:(t + 1) * P], x_st[:, b, t, :], ident[:, :])
                    last.then_inc(x1T_done, 1)
                    wait_count(pe, x1T_copied, n + 1)
                    for t in range(NB):
                        last = nc.tensor.matmul(kvq_ps(t // 2)[:, (t % 2) * 3 * D:(t % 2 + 1) * 3 * D], xT[:, b, t, :], w_kvq[:, :], start=True, stop=True)
                    last.then_inc(kvq_done, 1)
                    wait_count(pe, kvq_copied, n + 1)

            def turn_attr(q, b, g):
                if g == 0:
                    wait_count(pe, attr_loaded[b], (q + 1) * (2 * CG * 16))
                for u in range(GT):
                    last = nc.tensor.transpose(fwd[:, g % 2, u::GT], attr_in[:, b, g * GT + u, :], ident[:, :])
                last.then_inc(attrT_done, 1)

            def project(q, b, g):
                G = (q * 2 + b) * CG + g
                wait_count(pe, attrT_copied, G + 1)
                for u in range(GT):
                    nc.tensor.matmul(proj[:, g % 2, u * D:(u + 1) * D], attrT[:, g % 2, u * P:(u + 1) * P], w_e[:, :], start=True, stop=True)
                wait_count(pe, q_scanned, G + 2)
                for u in range(GT):
                    last = nc.tensor.transpose(proj[:, g % 2, (GT + u) * D:(GT + u + 1) * D],
                                               sums[D:2 * D, b, g * GE + u:(g + 1) * GE:GT], ident[D:2 * D, D:2 * D])
                last.then_inc(eproj_done, 1)

            def turn_message(q, b, g):
                wait_count(pe, kv_used, (q * 2 + b) * CG + g + 1 + FREE_G)
                for u in range(GT):
                    last = nc.tensor.transpose(fwd[0:D, 2 + g % 2, u::GT], msg[:, g, u, :], ident[:, :])
                last.then_inc(S_ATT.fwd_done, 1)

            def att_products(i, first, last):
                for g in range(PG):
                    if not (first and g < 1):
                        turn_message(*att_group(i, g - 1))
                    if not (first and g < 2):
                        turn_back(S_ATT, *att_group(i, g - 2))
                    if not (last and g + 2 >= PG):
                        turn_attr(*att_group(i, g + 2))
                    if not (last and g + 1 >= PG):
                        project(*att_group(i, g + 1))

            for g in range(2):
                turn_attr(0, 0, g)
            project(0, 0, 0)
            att_pairs(pe, att_products)
            turn_message(*att_group(PAIRS, -1))
            for g in range(2):
                turn_back(S_ATT, *att_group(PAIRS, g - 2))


_INS = ['x', 'src', 'dst', 'edge_attr_64', 'edge_weight', 'L1_gnn_WQ', 'L1_gnn_bQ', 'L1_gnn_WK', 'L1_gnn_bK',
        'L1_gnn_WE', 'L1_gnn_bE', 'L1_gnn_WV', 'L1_gnn_bV']
_OUTS = [((12500, 64), 'float32')]


def kernel(**inputs):
    import numpy as _np
    import concourse.bacc as _bacc
    from concourse import mybir as _mybir
    from concourse.bass_utils import run_bass_kernel_spmd as _run

    nc = _bacc.Bacc("TRN2", target_bir_lowering=False, num_devices=1)
    arrays, args = {}, []
    for name in _INS:
        a = _np.ascontiguousarray(inputs[name])
        arrays[f"in_{name}_dram"] = a
        args.append(nc.dram_tensor(f"in_{name}_dram", a.shape, _mybir.dt.from_np(a.dtype), kind="ExternalInput").ap())
    for i, (shape, dtype) in enumerate(_OUTS):
        dt = _mybir.dt.from_np(_np.dtype(dtype))
        args.append(nc.dram_tensor(f"out_{i}_dram", shape, dt, kind="ExternalOutput").ap())
    build(nc, *args)
    r = _run(nc, [arrays], core_ids=[0])
    got = tuple(r.results[0][f"out_{i}_dram"] for i in range(len(_OUTS)))
    return got[0]
```
